# Optimizing a Trainium2 kernel written in Bass

```python
import numpy as np
import jax
import jax.numpy as jnp

def _softmax(x, axis=-1):
    return jax.nn.softmax(x, axis=axis)

def _gelu(x):
    return jax.nn.gelu(x, approximate=True)

def _silu(x):
    return jax.nn.silu(x)

def _sigmoid(x):
    return jax.nn.sigmoid(x)

def _layernorm(x, axis=-1, eps=1e-05):
    m = jnp.mean(x, axis=axis, keepdims=True)
    v = jnp.var(x, axis=axis, keepdims=True)
    return (x - m) / jnp.sqrt(v + eps)

def _scatter_add(tgt, idx, src, axis=0):
    return tgt.at[idx].add(src)

def _segment_sum(src, seg, n):
    return jax.ops.segment_sum(src, seg, n)
kernel_name = 'mk_xattn_ffn_d1_seqx_r8_cd3f0d'

def setup_inputs(seed: int=0):
    np.random.seed(seed)
    _w = jnp.asarray

    def _rec_inputs():
        import jax
        import jax.numpy as jnp
        _rk = jax.random.key(seed)
        x = -0.000125 + 0.9999 * jax.random.normal(jax.random.fold_in(_rk, 1), (4, 256, 256), jnp.float32)
        _lenS = 256 - jax.random.randint(jax.random.fold_in(_rk, 7), (4,), 0, max(1, 256 // 4) + 1, jnp.int32)
        _lenS2 = 256 - jax.random.randint(jax.random.fold_in(_rk, 8), (4,), 0, max(1, 256 // 4) + 1, jnp.int32)
        itok_BxS_13_99985 = jax.random.randint(jax.random.fold_in(_rk, 11), (4, 256), 13, 99986, jnp.int32)
        _ctx_2048P = jax.random.normal(jax.random.fold_in(_rk, 12), (4, 16, 256), jnp.float32)
        _ctx_2048c = jax.random.dirichlet(jax.random.fold_in(_rk, 512), 0.3 * jnp.ones((16,), jnp.float32), (4, 256))
        _ctx_2048t = jnp.einsum('bsk,bkd->bsd', _ctx_2048c, _ctx_2048P)
        _ctx_2048t = _ctx_2048t * jax.lax.rsqrt(jnp.mean(jnp.square(_ctx_2048t)) + 1e-12) * 0.953939
        ctx_2048 = 6.82029e-06 + 0.0200006 * (_ctx_2048t + 0.3 * jax.random.normal(jax.random.fold_in(_rk, 612), (4, 256, 256), jnp.float32))
        return (x, itok_BxS_13_99985, ctx_2048)
    x, itok_BxS_13_99985, ctx_2048 = _rec_inputs()

    def _L0_xattn_setup():
        import jax, jax.numpy as jnp
        import numpy as np
        B, S, D = (4, 512, 256)
        E = 4
        F = 1024 // E
        VOCAB = 12500
        key = jax.random.key(seed)
        k1, k2, k3, k4, k5 = jax.random.split(key, 5)
        hidden_states = jax.random.normal(k1, (B, S, D), dtype=jnp.float32)
        token_ids = jax.random.randint(k2, (B, S), 0, VOCAB, dtype=jnp.int64)
        Wg = jax.random.normal(k3, (E, F, D), dtype=jnp.float32) * 0.02
        Wu = jax.random.normal(k4, (E, F, D), dtype=jnp.float32) * 0.02
        Wd = jax.random.normal(k5, (E, D, F), dtype=jnp.float32) * 0.02
        return {'hidden_states': hidden_states, 'token_ids': token_ids, 'Wg': Wg, 'Wu': Wu, 'Wd': Wd}
    _L0_xattn_all = _L0_xattn_setup()
    _L0_xattn_in = {k: v for k, v in _L0_xattn_all.items() if k in ()}
    del _L0_xattn_all

    def _L0_ffn_setup():
        import jax, jax.numpy as jnp
        import numpy as np
        HIDDEN = 256
        MOE_INTER = 128
        SHARED_INTER = 512
        N_EXPERTS = 16
        TOP_K = 2
        N_GROUP = 4
        TOPK_GROUP = 2
        NORM_TOPK_PROB = True
        ROUTED_SCALING = 1.0

        def relu2(x):
            r = jax.nn.relu(x)
            return r * r

        def _get_topk_indices(scores, e_bias):
            T, E = scores.shape
            s = scores + e_bias[None, :]
            gsz = E // N_GROUP
            group_scores = jax.lax.top_k(s.reshape(T, N_GROUP, gsz), 2)[0].sum(-1)
            group_idx = jax.lax.top_k(group_scores, TOPK_GROUP)[1]
            group_mask = jnp.zeros((T, N_GROUP), dtype=bool).at[jnp.arange(T)[:, None], group_idx].set(True)
            score_mask = jnp.repeat(group_mask, gsz, axis=1)
            masked = jnp.where(score_mask, s, 0.0)
            topk_indices = jax.lax.top_k(masked, TOP_K)[1]
            return jax.lax.stop_gradient(topk_indices)

        def _router(x_flat, router_weight, e_bias):
            logits = jnp.einsum('th,eh->te', x_flat.astype(jnp.float32), router_weight.astype(jnp.float32))
            scores = jax.nn.sigmoid(logits)
            topk_indices = _get_topk_indices(scores, e_bias)
            topk_weights = jnp.take_along_axis(scores, topk_indices, axis=1)
            if NORM_TOPK_PROB:
                topk_weights = topk_weights / (topk_weights.sum(-1, keepdims=True) + 1e-20)
            return (topk_indices, topk_weights * ROUTED_SCALING)
        key = jax.random.key(seed)
        ks = jax.random.split(key, 6)
        s = 0.02
        hidden_states = jax.random.normal(ks[0], (1, 256, HIDDEN), dtype=jnp.float32)
        router_weight = jax.random.normal(ks[1], (N_EXPERTS, HIDDEN), dtype=jnp.float32) * s
        e_bias = jnp.zeros((N_EXPERTS,), dtype=jnp.float32)
        w_up = jax.random.normal(ks[2], (N_EXPERTS, HIDDEN, MOE_INTER), dtype=jnp.float32) * s
        w_down = jax.random.normal(ks[3], (N_EXPERTS, MOE_INTER, HIDDEN), dtype=jnp.float32) * s
        shared_up = jax.random.normal(ks[4], (HIDDEN, SHARED_INTER), dtype=jnp.float32) * s
        shared_down = jax.random.normal(ks[5], (SHARED_INTER, HIDDEN), dtype=jnp.float32) * s
        return {'hidden_states': hidden_states, 'router_weight': router_weight, 'e_bias': e_bias, 'w_up': w_up, 'w_down': w_down, 'shared_up': shared_up, 'shared_down': shared_down}
    _L0_ffn_all = _L0_ffn_setup()
    _L0_ffn_in = {k: v for k, v in _L0_ffn_all.items() if k in ('router_weight', 'e_bias', 'w_up', 'w_down', 'shared_up', 'shared_down')}
    del _L0_ffn_all
    return {'x': x, 'itok_BxS_13_99985': itok_BxS_13_99985, 'ctx_2048': ctx_2048, 'L0_ffn_router_weight': _L0_ffn_in['router_weight'], 'L0_ffn_e_bias': _L0_ffn_in['e_bias'], 'L0_ffn_w_up': _L0_ffn_in['w_up'], 'L0_ffn_w_down': _L0_ffn_in['w_down'], 'L0_ffn_shared_up': _L0_ffn_in['shared_up'], 'L0_ffn_shared_down': _L0_ffn_in['shared_down']}

def reference(x, itok_BxS_13_99985, ctx_2048, L0_ffn_router_weight, L0_ffn_e_bias, L0_ffn_w_up, L0_ffn_w_down, L0_ffn_shared_up, L0_ffn_shared_down):
    import jax
    import jax.numpy as jnp

    def _L0_xattn_ref(hidden_states, token_ids, Wg, Wu, Wd):
        import jax, jax.numpy as jnp
        import numpy as np
        B, S, D = (4, 512, 256)
        E = 4
        F = 1024 // E
        VOCAB = 12500
        tokens_per_expert = VOCAB // E
        tid = jnp.clip(token_ids, 0, VOCAB - 1)
        expert_ids = jnp.minimum(tid // tokens_per_expert, E - 1)
        out = jnp.zeros_like(hidden_states)
        for e in range(E):
            g = jax.nn.silu(jnp.einsum('bsd,fd->bsf', hidden_states, Wg[e]))
            u = jnp.einsum('bsd,fd->bsf', hidden_states, Wu[e])
            y = jnp.einsum('bsf,df->bsd', g * u, Wd[e])
            out = jnp.where((expert_ids == e)[..., None], y, out)
        return out

    def _L0_ffn_ref(hidden_states, router_weight, e_bias, w_up, w_down, shared_up, shared_down):
        import jax, jax.numpy as jnp
        import numpy as np
        HIDDEN = 256
        MOE_INTER = 128
        SHARED_INTER = 512
        N_EXPERTS = 16
        TOP_K = 2
        N_GROUP = 4
        TOPK_GROUP = 2
        NORM_TOPK_PROB = True
        ROUTED_SCALING = 1.0

        def relu2(x):
            r = jax.nn.relu(x)
            return r * r

        def _get_topk_indices(scores, e_bias):
            T, E = scores.shape
            s = scores + e_bias[None, :]
            gsz = E // N_GROUP
            group_scores = jax.lax.top_k(s.reshape(T, N_GROUP, gsz), 2)[0].sum(-1)
            group_idx = jax.lax.top_k(group_scores, TOPK_GROUP)[1]
            group_mask = jnp.zeros((T, N_GROUP), dtype=bool).at[jnp.arange(T)[:, None], group_idx].set(True)
            score_mask = jnp.repeat(group_mask, gsz, axis=1)
            masked = jnp.where(score_mask, s, 0.0)
            topk_indices = jax.lax.top_k(masked, TOP_K)[1]
            return jax.lax.stop_gradient(topk_indices)

        def _router(x_flat, router_weight, e_bias):
            logits = jnp.einsum('th,eh->te', x_flat.astype(jnp.float32), router_weight.astype(jnp.float32))
            scores = jax.nn.sigmoid(logits)
            topk_indices = _get_topk_indices(scores, e_bias)
            topk_weights = jnp.take_along_axis(scores, topk_indices, axis=1)
            if NORM_TOPK_PROB:
                topk_weights = topk_weights / (topk_weights.sum(-1, keepdims=True) + 1e-20)
            return (topk_indices, topk_weights * ROUTED_SCALING)
        orig_shape = hidden_states.shape
        x = hidden_states.reshape(-1, HIDDEN)
        T = x.shape[0]
        topk_indices, topk_weights = _router(x, router_weight, e_bias)
        combine = jnp.zeros((T, N_EXPERTS), dtype=topk_weights.dtype).at[jnp.arange(T)[:, None], topk_indices].add(topk_weights)
        h1 = jnp.einsum('th,ehi->tei', x, w_up)
        a = relu2(h1) * combine[:, :, None]
        routed = jnp.einsum('tei,eih->th', a, w_down)
        shared = relu2(hidden_states @ shared_up) @ shared_down
        return routed.reshape(orig_shape) + shared
    x = x + _L0_xattn_ref(_layernorm(x, axis=-1), itok_BxS_13_99985, ctx_2048, ctx_2048, ctx_2048)
    x = x + _L0_ffn_ref(_layernorm(x, axis=-1), L0_ffn_router_weight, L0_ffn_e_bias, L0_ffn_w_up, L0_ffn_w_down, L0_ffn_shared_up, L0_ffn_shared_down)
    return x

_drawn_inputs = setup_inputs


def setup_inputs(seed=0):
    import zlib

    import numpy as np

    out = dict(_drawn_inputs(seed))
    spreads = {'L0_ffn_e_bias': (0.0, 0.334)}
    factors = {'L0_ffn_router_weight': 4.355, 'L0_ffn_w_up': 3.074, 'L0_ffn_w_down': 2.814}
    for name, (base, spread) in spreads.items():
        noise = np.random.default_rng([zlib.crc32(name.encode()), seed]).standard_normal(out[name].shape)
        drawn = base * np.exp(spread * noise) if base else spread * noise
        out[name] = jnp.asarray(drawn.astype(out[name].dtype))
    for name, factor in factors.items():
        out[name] = (out[name] * factor).astype(out[name].dtype)
    return out
```

```python
import concourse.bass as bass
from concourse import mybir
from contextlib import ExitStack

F32, F32R, BF16, I32 = mybir.dt.float32, mybir.dt.float32r, mybir.dt.bfloat16, mybir.dt.int32
ALU, ACT = mybir.AluOpType, mybir.ActivationFunctionType
AXX = mybir.AxisListType.X

P = 128
TOKENS, D = 1024, 256
KB = D // P
NT = TOKENS // P
CHUNKS, CT = 2, 4
CW = CT * P
E1, F1, VOCAB = 4, 256, 12500
PER_EXPERT = VOCAB // E1
E2, F2, K2 = 16, 128, 2
GROUPS, GE = 4, 4
SH = 512
SB = SH // P
EPS = 1e-5
ROW = D + 2
SLOT_TILES = (K2 * TOKENS - E2) // P + E2
OUT_OF_BOUNDS = 4096
NXS = 4
STEPS = CHUNKS * E1
NBLK = 2 * STEPS
NG = 8
FIRST = 7
MAIN = (SLOT_TILES - FIRST) // NXS


def build(nc, x, token_ids, ctx_w, router_w, e_bias, w_up, w_down, shared_up, shared_down, out):
    ctx = ExitStack()
    with ctx:
        def sb(name, shape, dt=F32):
            return ctx.enter_context(nc.sbuf_tensor(name, shape, dt))

        def sem(name):
            return ctx.enter_context(nc.semaphore(name))

        slots = nc.dram_tensor("slots", [(SLOT_TILES + 1) * P, ROW], F32, kind="Internal").ap()
        routed = nc.dram_tensor("routed", [K2 * TOKENS, D], F32, kind="Internal").ap()

        X = sb("X", [P, NT, D])
        rows = sb("rows", [P, NT * K2 * ROW])
        rows_v = rows[:, :].rearrange("p (t k r) -> p t k r", t=NT, k=K2)
        back = rows[:, 0:NT * K2 * D].rearrange("p (t r) -> p t r", t=NT)
        XThi = sb("XThi", [P, KB, TOKENS], F32R)
        XTlo = sb("XTlo", [P, KB, TOKENS], F32R)
        ctx_raw = sb("ctx_raw", [P, E1 * KB, D])
        WThi = sb("WThi", [P, E1, KB, F1], F32R)
        WTlo = sb("WTlo", [P, E1, KB, F1], F32R)
        rw_raw = sb("rw_raw", [E2, D])
        RWhi = sb("RWhi", [P, KB, E2], F32R)
        RWlo = sb("RWlo", [P, KB, E2], F32R)
        bias = sb("bias", [P, E2])
        su_raw = sb("su_raw", [P, KB, SH])
        SUhi = sb("SUhi", [P, KB, SH], F32R)
        SUlo = sb("SUlo", [P, KB, SH], F32R)
        sd_raw = sb("sd_raw", [P, SB, D])
        SDhi = sb("SDhi", [P, SB, D], F32R)
        SDlo = sb("SDlo", [P, SB, D], F32R)
        WU = sb("WU", [P, E2 * KB * F2])
        WD = sb("WD", [P, E2 * D])
        ids = sb("ids", [P, TOKENS], I32)
        code = sb("code", [P, TOKENS], BF16)
        sg = sb("sg", [P, 4, CW])
        sq = sb("sq", [P, 2, CW])
        act1 = sb("act1", [P, 4, CW])
        Ghi = sb("Ghi", [P, NG, CW], F32R)
        Glo = sb("Glo", [P, NG, CW], F32R)
        yTs = sb("yTs", [P, KB, CW])
        stats = sb("stats", [P, NT, 6])
        mv = sb("mv", [P, NT, 2])
        rstd = sb("rstd", [P, NT])
        var = sb("var", [P, NT])
        minus_half_var = sb("minus_half_var", [P, NT])
        guess = sb("guess", [P, NT], I32)
        XS = sb("XS", [P, NXS, ROW])
        XSd = [XS[:, b, D + 1:D + 2].bitcast(I32) for b in range(NXS)]
        XST = sb("XST", [P, 2, D])
        R = sb("R", [P, 2, F2])
        A = sb("A", [P, 2, F2])
        AT = sb("AT", [P, 2, P])
        Y = sb("Y", [P, NXS, D])
        dest = sb("dest", [P, NXS], I32)
        ident = sb("ident", [P, P])
        before = sb("before", [P, P], BF16)
        ones = sb("ones", [P, P], BF16)
        lower_group = sb("lower_group", [P, GROUPS, GROUPS])
        e_left = sb("e_left", [P, E2])
        starts = sb("starts", [P, NT])
        tile_no = sb("tile_no", [1, 32])
        pad_row = sb("pad_row", [P, ROW])
        warm = sb("warm", [P, 1])
        ones_f = sb("ones_f", [P, E2])
        SC = sb("SC", [P, NT, E2])
        biased = sb("biased", [P, NT, E2])
        pairs = sb("pairs", [P, NT * GROUPS, 6])
        gscore = sb("gscore", [P, NT, GROUPS])
        beats = sb("beats", [P, NT, GROUPS, GROUPS])
        ties = sb("ties", [P, NT, GROUPS, GROUPS])
        grank = sb("grank", [P, NT, GROUPS])
        masked = sb("masked", [P, K2, NT, E2])
        best = sb("best", [P, K2, NT])
        cand = sb("cand", [P, K2, NT, E2])
        hit = sb("hit", [P, K2, NT, E2])
        chosen = sb("chosen", [P, NT, E2], BF16)
        pv = sb("pv", [P, K2, NT])
        psum_w = sb("psum_w", [P, NT])
        count = sb("count", [P, E2])
        over = sb("over", [P, E2, NT])
        tiles_of = sb("tiles_of", [P, E2])
        tiles_to = sb("tiles_to", [P, E2])
        first = sb("first", [P, E2])
        place = sb("place", [P, NT, E2])
        spot = sb("spot", [P, K2, NT])
        spot_i = sb("spot_i", [P, K2, NT], I32)
        past = yTs[0:1, 0, :].rearrange("p (n e) -> p n e", e=E2)
        texp = sb("texp", [1, 32])
        texp_i = sb("texp_i", [1, 32], I32)

        misc = [ctx.enter_context(nc.psum_tensor(f"misc{i}", [P, CW], F32)) for i in range(2)]
        H = [ctx.enter_context(nc.psum_tensor(f"H{i}", [P, CW], F32)) for i in range(4)]
        YT = [ctx.enter_context(nc.psum_tensor(f"YT{i}", [P, CW], F32)) for i in range(2)]

        x_in = [sem(f"x_in{c}") for c in range(CHUNKS)]
        ids_in, ctx_in, rw_in, bias_in = sem("ids_in"), sem("ctx_in"), sem("rw_in"), sem("bias_in")
        su_in, sd_in, wu_in, wd_in = sem("su_in"), sem("sd_in"), sem("wu_in"), sem("wd_in")
        pads_out = sem("pads_out")
        consts = sem("consts")
        dve_chain = sem("dve_chain")
        normed = sem("normed")
        coded = sem("coded")
        moved = sem("moved")
        hi_done = sem("hi_done")
        misc_free = sem("misc_free")
        whi_done = sem("whi_done")
        wlo_done = sem("wlo_done")
        h_ready = sem("h_ready")
        sq_done = sem("sq_done")
        act_ready = sem("act_ready")
        ghi_done, glo_done = sem("ghi_done"), sem("glo_done")
        y_done = sem("y_done")
        yT_saved = sem("yT_saved")
        scored = sem("scored")
        chosen_ready = sem("chosen_ready")
        spots_ready = sem("spots_ready")
        texp_ready = sem("texp_ready")
        sd_ready = sem("sd_ready")
        sd_added = sem("sd_added")
        rows_out = sem("rows_out")
        xs_in = [sem(f"xs_in{b}") for b in range(NXS)]
        y_out = [sem(f"y_out{b}") for b in range(NXS)]
        xt_ready, xt_saved = sem("xt_ready"), sem("xt_saved")
        up_ready, r_ready, a_ready = sem("up_ready"), sem("r_ready"), sem("a_ready")
        at_ready, at_saved = sem("at_ready"), sem("at_saved")
        down_ready, y_saved = sem("down_ready"), sem("y_saved")
        dest_ready = sem("dest_ready")
        scatters_begun = sem("scatters_begun")
        back_in = [sem(f"back_in{c}") for c in range(4)]
        out_ready = sem("out_ready")
        out_done = sem("out_done")

        U_X = [[0, 1], [6, 7]]
        U_W = [2, 3, 4, 5]
        U_RW = 8
        U_BACK = [[9, 10], [14, 15]]
        U_X2 = [[11, 12], [16, 17]]
        U_ROUTE = [13, 18]
        U_RANK = 19
        SPLITS = [0, 1, 2, 3, 4, 5, 6, 7, 8, 11, 12, 16, 17]

        x_t = x.rearrange("b (s p) d -> p (b s) d", p=P)
        out_t = out.rearrange("b (s p) d -> p (b s) d", p=P)
        routed_t = routed.rearrange("(t p k) d -> p t (k d)", p=P, k=K2)
        slots_t = slots.rearrange("(n p) r -> n p r", p=P)

        block = ctx.enter_context(nc.Block())

        @block.sync
        def _(sp):
            for c in range(CHUNKS):
                sp.dma_start(X[:, c * CT:(c + 1) * CT, :], x_t[:, c * CT:(c + 1) * CT, :]).then_inc(x_in[c], 16)
            sp.dma_start(su_raw[:], shared_up.rearrange("(k p) n -> p k n", p=P)).then_inc(su_in, 16)
            sp.dma_start(sd_raw[:], shared_down.rearrange("(k p) n -> p k n", p=P)).then_inc(sd_in, 16)
            sp.dma_start(WU[:].rearrange("p (e k f) -> p e k f", e=E2, k=KB),
                         w_up.rearrange("e (k p) f -> p e k f", p=P)).then_inc(wu_in, 16)
            sp.dma_start(WD[:].rearrange("p (e d) -> p e d", e=E2),
                         w_down.rearrange("e p d -> p e d")).then_inc(wd_in, 16)
            sp.wait_ge(rows_out, 16 * K2 * NT)

            def load(n_of, b):
                sp.dma_start(XS[:, b, :], n_of).then_inc(xs_in[b], 16)

            for b in range(NXS):
                load(slots_t[b], b)
            with sp.Fori(1, (SLOT_TILES + 1) // NXS) as i:
                for b in range(NXS):
                    sp.wait_ge(a_ready, NXS * i + (b - NXS + 1))
                    sp.wait_ge(dest_ready, NXS * i + (b - NXS + 1))
                    sp.dma_start(XS[:, b, :], slots[bass.ds(NXS * P * i + b * P, P), :]).then_inc(xs_in[b], 16)
            for b in range(NXS):
                sp.wait_ge(y_out[b], 16 * ((SLOT_TILES - 1 - b) // NXS + 1))
            for q in range(4):
                sp.dma_start(back[:, 2 * q:2 * q + 2, :], routed_t[:, 2 * q:2 * q + 2, :]).then_inc(back_in[q], 16)
            for q in range(4):
                sp.wait_ge(out_ready, q + 1)
                sp.dma_start(out_t[:, 2 * q:2 * q + 2, :], X[:, 2 * q:2 * q + 2, :]).then_inc(out_done, 16)
            sp.wait_ge(out_done, 16 * 4)
            sp.wait_ge(pads_out, 16)

        @block.gpsimd
        def _(pool):
            n = [0]

            def const(ins):
                n[0] += 1
                ins.then_inc(consts, 1)

            const(pool.memset(ident[:], 0.0))
            const(pool.memset(before[:], 1.0))
            const(pool.memset(lower_group[:], 1.0))
            const(pool.memset(pad_row[:], 0.0))
            const(pool.memset(ones[:], 1.0))
            const(pool.memset(ones_f[:], 1.0))
            pool.wait_ge(consts, n[0])
            const(pool.affine_select(out=ident[:], in_=ident[:], compare_op=ALU.not_equal, fill=1.0, base=0,
                                     pattern=[[-1, P]], channel_multiplier=1))
            const(pool.affine_select(out=before[:], in_=before[:], compare_op=ALU.is_gt, fill=0.0, base=0,
                                     pattern=[[1, P]], channel_multiplier=-1))
            const(pool.affine_select(out=lower_group[:], in_=lower_group[:], compare_op=ALU.is_gt, fill=0.0,
                                     base=0, pattern=[[1, GROUPS], [-1, GROUPS]], channel_multiplier=0))
            const(pool.memset(pad_row[:, D + 1:D + 2].bitcast(I32), OUT_OF_BOUNDS))
            const(pool.iota(e_left[:], pattern=[[-1, E2]], base=E2, channel_multiplier=0,
                            allow_small_or_imprecise_dtypes=True))
            const(pool.iota(starts[:], pattern=[[P, NT]], base=0, channel_multiplier=0,
                            allow_small_or_imprecise_dtypes=True))
            const(pool.iota(tile_no[:], pattern=[[1, 32]], base=0, channel_multiplier=0,
                            allow_small_or_imprecise_dtypes=True))
            pool.wait_ge(consts, n[0])
            pool.dma_start(slots.rearrange("(n p) r -> p n r", p=P),
                           pad_row[:].unsqueeze(1).broadcast_to([P, SLOT_TILES + 1, ROW])).then_inc(pads_out, 16)
            const(pool.iota(rows_v[:, :, :, D + 1:D + 2].bitcast(I32),
                            pattern=[[K2 * P, NT], [1, K2], [0, 1]], base=0, channel_multiplier=K2))
            assert n[0] == 14
            pool.wait_ge(pads_out, 16)
            pool.wait_ge(consts, 14)
            pool.wait_ge(spots_ready, 1)
            for t in range(NT):
                for k in range(K2):
                    pool.indirect_dma_start(
                        slots, bass.IndirectOffsetOnAxis(ap=spot_i[:, k, t:t + 1], axis=0),
                        rows_v[:, t, k, :], None, bounds_check=(SLOT_TILES + 1) * P - 1,
                        oob_is_err=False).then_inc(rows_out, 16)

            def scatter(b, n):
                pool.wait_ge(y_saved, n + 1)
                pool.wait_ge(dest_ready, n + 1)
                pool.sem_inc(scatters_begun, 1)
                pool.indirect_dma_start(
                    routed, bass.IndirectOffsetOnAxis(ap=dest[:, b:b + 1], axis=0),
                    Y[:, b, :], None, bounds_check=K2 * TOKENS - 1, oob_is_err=False).then_inc(y_out[b], 16)

            with pool.Fori(0, SLOT_TILES // NXS) as i:
                for b in range(NXS):
                    scatter(b, NXS * i + b)
            for n_ in range(SLOT_TILES // NXS * NXS, SLOT_TILES):
                scatter(n_ % NXS, n_)

        @block.tensor
        def _(pe):
            def use(u):
                if u >= 2:
                    pe.wait_ge(misc_free, u - 1)
                return misc[u % 2]

            def transpose_x(c, kb, u, reader_sem, value):
                bank = use(u)
                pe.wait_ge(reader_sem, value)
                for j in range(CT):
                    last = pe.transpose(bank[:, j * P:(j + 1) * P],
                                        rows_v[:, c * CT + j, 0, kb * P:(kb + 1) * P], ident[:])
                last.then_inc(moved, 1)

            def transpose_w(e):
                bank = use(U_W[e])
                pe.wait_ge(ctx_in, 16)
                for kb in range(KB):
                    for ib in range(KB):
                        last = pe.transpose(bank[:, kb * F1 + ib * P:kb * F1 + (ib + 1) * P],
                                            ctx_raw[:, e * KB + ib, kb * P:(kb + 1) * P], ident[:])
                last.then_inc(moved, 1)

            def split_product(dst, pairs_of, sg_check=False):
                terms = [t for (ahi, alo, bhi, blo) in pairs_of for t in ((ahi, bhi), (ahi, blo), (alo, bhi))]
                for j, (a, b) in enumerate(terms):
                    last = pe.matmul(dst, a, b, start=(j == 0), stop=(j == len(terms) - 1))
                return last

            def hidden(s):
                c, e = divmod(s, E1)
                if e == 0:
                    for kb in range(KB):
                        u = SPLITS.index(U_X[c][kb]) + 1
                        pe.wait_ge(hi_done, u)
                        pe.wait_ge(misc_free, U_X[c][kb] + 1)
                pe.wait_ge(hi_done, SPLITS.index(U_W[e]) + 1)
                pe.wait_ge(misc_free, U_W[e] + 1)
                for b in range(2):
                    n = 2 * s + b
                    if n >= 4:
                        pe.wait_ge(sq_done, n - 3)
                    w = slice(b * P, (b + 1) * P)
                    cw = slice(c * CW, (c + 1) * CW)
                    split_product(H[n % 4][:], [(WThi[:, e, kb, w], WTlo[:, e, kb, w],
                                                 XThi[:, kb, cw], XTlo[:, kb, cw]) for kb in range(KB)]
                                  ).then_inc(h_ready, 1)

            def project(s):
                c, e = divmod(s, E1)
                if c and e == 0:
                    pe.wait_ge(yT_saved, 2 * c)
                for b in range(2):
                    n = 2 * s + b
                    pe.wait_ge(ghi_done, n + 1)
                    pe.wait_ge(glo_done, n + 1)
                    for db in range(KB):
                        w = slice(db * P, (db + 1) * P)
                        g = n % NG
                        terms = ((WThi, Ghi), (WThi, Glo), (WTlo, Ghi))
                        for j, (a, gg) in enumerate(terms):
                            last = pe.matmul(YT[db][:], a[:, e, b, w], gg[:, g, :],
                                             start=(e == 0 and b == 0 and j == 0),
                                             stop=(e == E1 - 1 and b == 1 and j == 2))
                last.then_inc(y_done, 1)

            def transpose_back(c):
                for half in range(2):
                    bank = use(U_BACK[c][half])
                    pe.wait_ge(yT_saved, 2 * c + 2)
                    for j in range(2):
                        for db in range(KB):
                            t = 2 * half + j
                            last = pe.transpose(bank[:, j * D + db * P:j * D + (db + 1) * P],
                                                yTs[:, db, t * P:(t + 1) * P], ident[:])
                    last.then_inc(moved, 1)

            def route(c):
                bank = use(U_ROUTE[c])
                for u in (U_X2[c][1], U_RW):
                    pe.wait_ge(hi_done, SPLITS.index(u) + 1)
                    pe.wait_ge(misc_free, u + 1)
                for j in range(CT):
                    tw = slice((c * CT + j) * P, (c * CT + j + 1) * P)
                    last = split_product(bank[:, j * E2:(j + 1) * E2],
                                         [(XThi[:, kb, tw], XTlo[:, kb, tw], RWhi[:, kb, :], RWlo[:, kb, :])
                                          for kb in range(KB)])
                last.then_inc(moved, 1)

            def shared_up_blocks(c, blocks):
                for ib in blocks:
                    n = NBLK + SB * c + ib
                    pe.wait_ge(whi_done, KB)
                    pe.wait_ge(wlo_done, KB)
                    pe.wait_ge(sq_done, n - 3)
                    w = slice(ib * P, (ib + 1) * P)
                    cw = slice(c * CW, (c + 1) * CW)
                    split_product(H[n % 4][:], [(SUhi[:, kb, w], SUlo[:, kb, w],
                                                 XThi[:, kb, cw], XTlo[:, kb, cw]) for kb in range(KB)]
                                  ).then_inc(h_ready, 1)

            def shared_down_tiles(c):
                pe.wait_ge(whi_done, KB + 2)
                pe.wait_ge(wlo_done, KB + 2)
                pe.wait_ge(yT_saved, 2 * CHUNKS)
                pe.wait_ge(ghi_done, NBLK + SB * (c + 1))
                pe.wait_ge(glo_done, NBLK + SB * (c + 1))
                for j in range(CT):
                    t = c * CT + j
                    if t >= 2:
                        pe.wait_ge(sd_added, t - 1)
                    tw = slice(j * P, (j + 1) * P)
                    g = [(NBLK + SB * c + ib) % NG for ib in range(SB)]
                    split_product(YT[t % 2][:, 0:D], [(Ghi[:, g[ib], tw], Glo[:, g[ib], tw],
                                                       SDhi[:, ib, :], SDlo[:, ib, :]) for ib in range(SB)]
                                  ).then_inc(sd_ready, 1)

            pe.wait_ge(consts, 14)
            for kb in range(KB):
                transpose_x(0, kb, U_X[0][kb], normed, CT)
            transpose_w(0)
            transpose_w(1)
            hidden(0)
            transpose_w(2)
            hidden(1)
            project(0)
            transpose_w(3)
            hidden(2)
            project(1)
            for kb in range(KB):
                transpose_x(1, kb, U_X[1][kb], normed, 2 * CT)
            bank = use(U_RW)
            pe.wait_ge(rw_in, 16)
            for kb in range(KB):
                last = pe.transpose(bank[:, kb * E2:(kb + 1) * E2], rw_raw[:, kb * P:(kb + 1) * P],
                                    ident[0:E2, 0:E2])
            last.then_inc(moved, 1)
            hidden(3)
            project(2)
            hidden(4)
            project(3)
            hidden(5)
            transpose_back(0)
            project(4)
            hidden(6)
            for kb in range(KB):
                transpose_x(0, kb, U_X2[0][kb], normed, 3 * CT)
            project(5)
            hidden(7)
            route(0)
            project(6)
            project(7)
            shared_up_blocks(0, (0, 1))
            transpose_back(1)
            shared_up_blocks(0, (2, 3))
            for kb in range(KB):
                transpose_x(1, kb, U_X2[1][kb], normed, 4 * CT)
            route(1)
            shared_up_blocks(1, range(SB))
            bank = use(U_RANK)
            pe.wait_ge(chosen_ready, CHUNKS)
            ranks = bank[:, 0:NT * E2]
            pe.matmul(ranks, before[:], chosen[:].rearrange("p t e -> p (t e)"), start=True, stop=False)
            for t in range(NT - 1):
                pe.matmul(bank[:, (t + 1) * E2:NT * E2].rearrange("p (t e) -> p t e", e=E2), ones[:],
                          chosen[:, t:t + 1, :].broadcast_to([P, NT - 1 - t, E2]),
                          start=False, stop=(t == NT - 2))
            for t in range(NT):
                last = pe.matmul(bank[:, NT * E2:(NT + 1) * E2], ones[:], chosen[:, t, :],
                                 start=(t == 0), stop=(t == NT - 1))
            last.then_inc(moved, 1)
            shared_down_tiles(0)
            shared_down_tiles(1)

            def slot_transpose(base, k):
                n = base + k
                pe.wait_ge(xs_in[k % NXS], NXS * n + (16 - NXS * (k % NXS)))
                if not (isinstance(base, int) and n < 2):
                    pe.wait_ge(xt_saved, n - 1)
                for kb in range(KB):
                    last = pe.transpose(misc[k % 2][:, kb * P:(kb + 1) * P],
                                        XS[:, k % NXS, kb * P:(kb + 1) * P], ident[:])
                last.then_inc(xt_ready, 1)

            def expert(n):
                return pe.value_load(texp_i[0:1, bass.ds(n, 1)], min_val=0, max_val=E2 - 1)

            def slot_up(base, k, e):
                n = base + k
                pe.wait_ge(xt_saved, n + 1)
                if not (isinstance(base, int) and n < 2):
                    pe.wait_ge(r_ready, n - 1)
                for kb in range(KB):
                    last = pe.matmul(H[k % 2][:, 0:F2], XST[:, k % 2, kb * P:(kb + 1) * P],
                                     WU[:, bass.ds(e * (KB * F2) + kb * F2, F2)],
                                     start=(kb == 0), stop=(kb == KB - 1))
                last.then_inc(up_ready, 1)

            def slot_act_transpose(base, k):
                n = base + k
                pe.wait_ge(a_ready, n + 1)
                if not (isinstance(base, int) and n < 2):
                    pe.wait_ge(at_saved, n - 1)
                pe.transpose(H[2 + k % 2][:, 0:P], A[:, k % 2, :], ident[:]).then_inc(at_ready, 1)

            def slot_down(base, k, e):
                n = base + k
                pe.wait_ge(at_saved, n + 1)
                if not (isinstance(base, int) and n < 2):
                    pe.wait_ge(y_saved, n - 1)
                pe.matmul(YT[k % 2][:, 0:D], AT[:, k % 2, :], WD[:, bass.ds(e * D, D)],
                          start=True, stop=True).then_inc(down_ready, 1)

            pe.wait_ge(misc_free, U_RANK + 1)
            pe.wait_ge(sd_added, NT)
            pe.wait_ge(sq_done, NBLK + CHUNKS * SB)
            pe.wait_ge(wu_in, 16)
            pe.wait_ge(wd_in, 16)
            pe.wait_ge(texp_ready, 1)
            slot_transpose(0, 0)
            slot_transpose(0, 1)
            e_last = expert(0)
            slot_up(0, 0, e_last)
            for n in range(1, FIRST):
                slot_transpose(0, n + 1)
                slot_act_transpose(0, n - 1)
                e_this = expert(n)
                slot_up(0, n, e_this)
                slot_down(0, n - 1, e_last)
                e_last = e_this
            with pe.Fori(0, MAIN) as i:
                e_last = expert(NXS * i + (FIRST - 1))
                for k in range(FIRST, FIRST + NXS):
                    slot_transpose(NXS * i, k + 1)
                    slot_act_transpose(NXS * i, k - 1)
                    e_this = expert(NXS * i + k)
                    slot_up(NXS * i, k, e_this)
                    slot_down(NXS * i, k - 1, e_last)
                    e_last = e_this
            slot_act_transpose(0, SLOT_TILES - 1)
            slot_down(0, SLOT_TILES - 1, expert(SLOT_TILES - 1))

        @block.scalar
        def _(act):
            act.dma_start(ctx_raw[:], ctx_w.rearrange("e (b p) d -> p (e b) d", p=P)).then_inc(ctx_in, 16)
            act.dma_start(ids[:], token_ids.rearrange("(o b) s -> o (b s)", o=1).broadcast_to([P, TOKENS])
                          ).then_inc(ids_in, 16)
            act.dma_start(rw_raw[:], router_w).then_inc(rw_in, 16)
            act.dma_start(bias[:], e_bias.rearrange("(o e) -> o e", o=1).broadcast_to([P, E2])
                          ).then_inc(bias_in, 16)

            def split_hi(u, dst):
                act.wait_ge(moved, u + 1)
                src = misc[u % 2][:]
                if len(dst.shape) == 3:
                    src = misc[u % 2][:, 0:dst.shape[1] * dst.shape[2]].rearrange("p (k n) -> p k n", k=dst.shape[1])
                nc.scalar.activation(dst, src, ACT.Copy).then_inc(hi_done, 1)

            def x_hi(c, uses):
                for kb in range(KB):
                    split_hi(uses[kb], XThi[:, kb, c * CW:(c + 1) * CW])

            def take(n, func):
                act.wait_ge(h_ready, n + 1)
                if n >= 4:
                    act.wait_ge(act_ready, n - 3)
                i = nc.scalar.activation(sg[:, n % 4, :], H[n % 4][:], func)
                if func == ACT.Relu:
                    i.then_inc(sq_done, 1)
                    return
                if n >= 2:
                    act.wait_ge(act_ready, n - 1)
                nc.scalar.activation(sq[:, n % 2, :], H[n % 4][:], ACT.Square).then_inc(sq_done, 1)

            def act_hi(n):
                act.wait_ge(act_ready, n + 1)
                if n >= NG:
                    act.wait_ge(y_done, (n - NG) // 2 + 1)
                nc.scalar.activation(Ghi[:, n % NG, :], act1[:, n % 4, :], ACT.Copy).then_inc(ghi_done, 1)

            def step(s):
                for b in range(2):
                    take(2 * s + b, ACT.Sigmoid)
                for b in range(2):
                    act_hi(2 * s + b)

            def save_y(c):
                act.wait_ge(y_done, E1 * (c + 1))
                if c:
                    act.wait_ge(moved, U_BACK[c - 1][1] + 1)
                for db in range(KB):
                    nc.scalar.activation(yTs[:, db, :], YT[db][:], ACT.Copy).then_inc(yT_saved, 1)

            def scores(c):
                act.wait_ge(moved, U_ROUTE[c] + 1)
                nc.scalar.activation(SC[:, c * CT:(c + 1) * CT, :],
                                     misc[U_ROUTE[c] % 2][:, 0:CT * E2].rearrange("p (t e) -> p t e", e=E2),
                                     ACT.Sigmoid).then_inc(scored, 1)

            x_hi(0, U_X[0])
            split_hi(U_W[0], WThi[:, 0])
            split_hi(U_W[1], WThi[:, 1])
            step(0)
            split_hi(U_W[2], WThi[:, 2])
            step(1)
            split_hi(U_W[3], WThi[:, 3])
            step(2)
            x_hi(1, U_X[1])
            split_hi(U_RW, RWhi[:])
            step(3)
            act.wait_ge(su_in, 16)
            for kb in range(KB):
                nc.scalar.activation(SUhi[:, kb, :], su_raw[:, kb, :], ACT.Copy).then_inc(whi_done, 1)
            step(4)
            save_y(0)
            act.wait_ge(sd_in, 16)
            for h in range(2):
                nc.scalar.activation(SDhi[:, 2 * h:2 * h + 2, :], sd_raw[:, 2 * h:2 * h + 2, :],
                                     ACT.Copy).then_inc(whi_done, 1)
            step(5)
            x_hi(0, U_X2[0])
            step(6)
            step(7)
            scores(0)
            save_y(1)
            for ib in range(SB):
                take(NBLK + ib, ACT.Relu)
            x_hi(1, U_X2[1])
            for ib in range(SB):
                act_hi(NBLK + ib)
            scores(1)
            for ib in range(SB):
                take(NBLK + SB + ib, ACT.Relu)
            for ib in range(SB):
                act_hi(NBLK + SB + ib)

            def slot_save_x(base, k):
                n = base + k
                act.wait_ge(xt_ready, n + 1)
                if not (isinstance(base, int) and n < 2):
                    act.wait_ge(up_ready, n - 1)
                nc.scalar.activation(XST[:, k % 2, :], misc[k % 2][:, 0:D], ACT.Copy).then_inc(xt_saved, 1)

            def slot_relu(base, k):
                n = base + k
                act.wait_ge(up_ready, n + 1)
                if not (isinstance(base, int) and n < 2):
                    act.wait_ge(a_ready, n - 1)
                nc.scalar.activation(R[:, k % 2, :], H[k % 2][:, 0:F2], ACT.Relu).then_inc(r_ready, 1)

            def slot_save_y(base, k):
                n = base + k
                act.wait_ge(down_ready, n + 1)
                if not (isinstance(base, int) and n < NXS):
                    act.wait_ge(y_out[k % NXS], NXS * n - NXS * (k % NXS))
                nc.scalar.activation(Y[:, k % NXS, :], YT[k % 2][:, 0:D], ACT.Copy).then_inc(y_saved, 1)

            slot_save_x(0, 0)
            slot_save_x(0, 1)
            slot_relu(0, 0)
            for n in range(1, FIRST):
                slot_save_x(0, n + 1)
                slot_relu(0, n)
                slot_save_y(0, n - 1)
            with act.Fori(0, MAIN) as i:
                for k in range(FIRST, FIRST + NXS):
                    slot_save_x(NXS * i, k + 1)
                    slot_relu(NXS * i, k)
                    slot_save_y(NXS * i, k - 1)
            slot_save_y(0, SLOT_TILES - 1)

        @block.vector
        def _(dve):
            chain = [0]

            def then(ins):
                chain[0] += 1
                ins.then_inc(dve_chain, 1)

            def settle():
                dve.wait_ge(dve_chain, chain[0])

            def link(ins):
                then(ins)
                settle()

            V = nc.vector

            def norm(c, copies):
                ts_ = range(c * CT, (c + 1) * CT)
                for t in ts_:
                    then(V.bn_stats(stats[:, t, :], X[:, t, :]))
                settle()
                for t in ts_:
                    then(V.bn_aggr(mv[:, t, :], stats[:, t, :]))
                settle()
                cs = slice(c * CT, (c + 1) * CT)
                y = rstd[:, cs]
                then(V.tensor_scalar(minus_half_var[:, cs], mv[:, cs, 1], EPS, -0.5, ALU.add, ALU.mult))
                link(V.tensor_scalar(var[:, cs], mv[:, cs, 1], EPS, None, ALU.add))
                link(V.tensor_scalar(guess[:, cs], var[:, cs].bitcast(I32), 1, None, ALU.arith_shift_right))
                link(V.tensor_scalar(y.bitcast(I32), guess[:, cs], -1.0, float(0x5F3759DF), ALU.mult, ALU.add))
                for _ in range(3):
                    link(V.tensor_tensor(var[:, cs], y, y, ALU.mult))
                    link(V.tensor_tensor(var[:, cs], var[:, cs], minus_half_var[:, cs], ALU.mult))
                    link(V.scalar_tensor_tensor(out=y, in0=var[:, cs], scalar=1.5, in1=y, op0=ALU.add, op1=ALU.mult))
                for t in ts_:
                    if copies == 1:
                        src, dst = X[:, t, :], rows_v[:, t, 0, 0:D]
                    else:
                        src = X[:, t:t + 1, :].broadcast_to([P, K2, D])
                        dst = rows_v[:, t, :, 0:D]
                    V.tensor_scalar(dst, src, mv[:, t, 0:1], rstd[:, t:t + 1], ALU.subtract,
                                    ALU.mult).then_inc(normed, 1)

            def split_lo(u, hi, lo):
                dve.wait_ge(hi_done, SPLITS.index(u) + 1)
                src = misc[u % 2][:]
                if len(hi.shape) == 3:
                    src = misc[u % 2][:, 0:hi.shape[1] * hi.shape[2]].rearrange("p (k n) -> p k n", k=hi.shape[1])
                V.tensor_tensor(lo, src, hi.bitcast(F32), ALU.subtract).then_inc(misc_free, 1)

            def x_lo(c, uses):
                for kb in range(KB):
                    cw = slice(c * CW, (c + 1) * CW)
                    split_lo(uses[kb], XThi[:, kb, cw], XTlo[:, kb, cw])

            def encode(c):
                if c == 0:
                    dve.wait_ge(ids_in, 16)
                cw = slice(c * CW, (c + 1) * CW)
                link(V.tensor_scalar(code[:, cw], ids[:, cw], float(PER_EXPERT), None, ALU.is_ge))
                for e in range(2, E1):
                    link(V.scalar_tensor_tensor(out=code[:, cw], in0=ids[:, cw], scalar=float(e * PER_EXPERT),
                                                in1=code[:, cw], op0=ALU.is_ge, op1=ALU.add))

            def act_lo(n):
                dve.wait_ge(ghi_done, n + 1)
                if n >= NG:
                    dve.wait_ge(y_done, (n - NG) // 2 + 1)
                V.tensor_tensor(Glo[:, n % NG, :], act1[:, n % 4, :], Ghi[:, n % NG, :].bitcast(F32),
                                ALU.subtract).then_inc(glo_done, 1)

            def step(s):
                c, e = divmod(s, E1)
                cw = slice(c * CW, (c + 1) * CW)
                for b in range(2):
                    n = 2 * s + b
                    dve.wait_ge(sq_done, n + 1)
                    then(V.scalar_tensor_tensor(out=sg[:, n % 4, :], in0=code[:, cw], scalar=float(e),
                                                in1=sg[:, n % 4, :], op0=ALU.is_equal, op1=ALU.mult))
                settle()
                for b in range(2):
                    n = 2 * s + b
                    if n >= 4:
                        dve.wait_ge(ghi_done, n - 3)
                        dve.wait_ge(glo_done, n - 3)
                    V.tensor_tensor(act1[:, n % 4, :], sg[:, n % 4, :], sq[:, n % 2, :],
                                    ALU.mult).then_inc(act_ready, 1)
                for b in range(2):
                    act_lo(2 * s + b)

            def shared_act(n):
                dve.wait_ge(sq_done, n + 1)
                dve.wait_ge(ghi_done, n - 3)
                dve.wait_ge(glo_done, n - 3)
                V.tensor_tensor(act1[:, n % 4, :], sg[:, n % 4, :], sg[:, n % 4, :], ALU.mult).then_inc(act_ready, 1)

            def add_back(c):
                for half in range(2):
                    u = U_BACK[c][half]
                    t = c * CT + 2 * half
                    dve.wait_ge(moved, u + 1)
                    V.tensor_tensor(X[:, t:t + 2, :].rearrange("p t d -> p (t d)"), misc[u % 2][:],
                                    X[:, t:t + 2, :].rearrange("p t d -> p (t d)"), ALU.add).then_inc(misc_free, 1)
                dve.wait_ge(misc_free, U_BACK[c][1] + 1)

            def choose(c):
                tw = slice(c * CT, (c + 1) * CT)
                gw = slice(c * CT * GROUPS, (c + 1) * CT * GROUPS)
                dve.wait_ge(scored, c + 1)
                link(V.tensor_tensor(biased[:, tw, :], SC[:, tw, :],
                                     bias[:].unsqueeze(1).broadcast_to([P, CT, E2]), ALU.add)
                     )
                s4 = biased[:, tw, :].rearrange("p t (g e) -> p (t g) e", g=GROUPS)
                then(V.tensor_tensor(pairs[:, gw, 0:3], s4[:, :, 0:3], s4[:, :, 1:4], ALU.add))
                then(V.tensor_tensor(pairs[:, gw, 3:5], s4[:, :, 0:2], s4[:, :, 2:4], ALU.add))
                link(V.tensor_tensor(pairs[:, gw, 5:6], s4[:, :, 0:1], s4[:, :, 3:4], ALU.add))
                gs = gscore[:, tw, :]
                link(V.tensor_reduce(gs.rearrange("p t g -> p (t g)"), pairs[:, gw, :], AXX, ALU.max))
                other = gs.unsqueeze(2).broadcast_to([P, CT, GROUPS, GROUPS])
                own = gs.unsqueeze(3).broadcast_to([P, CT, GROUPS, GROUPS])
                then(V.tensor_tensor(beats[:, tw], other, own, ALU.is_gt))
                link(V.tensor_tensor(ties[:, tw], other, own, ALU.is_equal))
                link(V.tensor_tensor(ties[:, tw], ties[:, tw],
                                     lower_group[:].unsqueeze(1).broadcast_to([P, CT, GROUPS, GROUPS]), ALU.mult))
                link(V.tensor_tensor(beats[:, tw], beats[:, tw], ties[:, tw], ALU.add))
                link(V.tensor_reduce(grank[:, tw, :], beats[:, tw], AXX, ALU.add))
                link(V.scalar_tensor_tensor(
                    out=masked[:, 0, tw, :].rearrange("p t (g e) -> p (t g) e", g=GROUPS),
                    in0=grank[:, tw, :].rearrange("p t g -> p (t g)").unsqueeze(2).broadcast_to([P, CT * GROUPS, GE]),
                    scalar=2.0, in1=s4, op0=ALU.is_lt, op1=ALU.mult))
                for k in range(K2):
                    m = masked[:, k, tw, :]
                    link(V.tensor_reduce(best[:, k, tw], m, AXX, ALU.max))
                    link(V.tensor_tensor(cand[:, k, tw, :], m, best[:, k, tw].unsqueeze(2).broadcast_to([P, CT, E2]),
                                         ALU.is_equal))
                    el = e_left[:].unsqueeze(1).broadcast_to([P, CT, E2])
                    link(V.tensor_tensor(cand[:, k, tw, :], cand[:, k, tw, :], el, ALU.mult))
                    link(V.tensor_reduce(best[:, k, tw], cand[:, k, tw, :], AXX, ALU.max))
                    link(V.tensor_tensor(hit[:, k, tw, :], el, best[:, k, tw].unsqueeze(2).broadcast_to([P, CT, E2]),
                                         ALU.is_equal))
                    if k == 0:
                        link(V.scalar_tensor_tensor(out=masked[:, 1, tw, :], in0=hit[:, 0, tw, :], scalar=-3e38,
                                                    in1=m, op0=ALU.mult, op1=ALU.add))
                V.tensor_tensor(chosen[:, tw, :], hit[:, 0, tw, :], hit[:, 1, tw, :], ALU.add
                                ).then_inc(chosen_ready, 1)

            def weigh(c):
                tw = slice(c * CT, (c + 1) * CT)
                link(V.tensor_tensor(cand[:, :, tw, :], hit[:, :, tw, :],
                                     SC[:, tw, :].unsqueeze(1).broadcast_to([P, K2, CT, E2]), ALU.mult))
                link(V.tensor_reduce(pv[:, :, tw], cand[:, :, tw, :], AXX, ALU.add))
                link(V.scalar_tensor_tensor(out=psum_w[:, tw], in0=pv[:, 0, tw], scalar=1.0, in1=pv[:, 1, tw],
                                            op0=ALU.mult, op1=ALU.add))
                link(V.tensor_scalar(psum_w[:, tw], psum_w[:, tw], 1e-20, None, ALU.add))
                link(V.reciprocal(psum_w[:, tw], psum_w[:, tw]))
                for k in range(K2):
                    then(V.tensor_tensor(rows_v[:, tw, k, D], pv[:, k, tw], psum_w[:, tw], ALU.mult))

            dve.wait_ge(x_in[0], 16)
            norm(0, 1)
            encode(0)
            x_lo(0, U_X[0])
            split_lo(U_W[0], WThi[:, 0], WTlo[:, 0])
            split_lo(U_W[1], WThi[:, 1], WTlo[:, 1])
            step(0)
            split_lo(U_W[2], WThi[:, 2], WTlo[:, 2])
            dve.wait_ge(x_in[1], 16)
            norm(1, 1)
            step(1)
            split_lo(U_W[3], WThi[:, 3], WTlo[:, 3])
            encode(1)
            step(2)
            x_lo(1, U_X[1])
            split_lo(U_RW, RWhi[:], RWlo[:])
            step(3)
            for kb in range(KB):
                dve.wait_ge(whi_done, kb + 1)
                V.tensor_tensor(SUlo[:, kb, :], su_raw[:, kb, :], SUhi[:, kb, :].bitcast(F32),
                                ALU.subtract).then_inc(wlo_done, 1)
            step(4)
            add_back(0)
            norm(0, 2)
            step(5)
            x_lo(0, U_X2[0])
            step(6)
            for h in range(2):
                dve.wait_ge(whi_done, KB + h + 1)
                V.tensor_tensor(SDlo[:, 2 * h:2 * h + 2, :], sd_raw[:, 2 * h:2 * h + 2, :],
                                SDhi[:, 2 * h:2 * h + 2, :].bitcast(F32), ALU.subtract).then_inc(wlo_done, 1)
            step(7)
            dve.wait_ge(bias_in, 16)
            dve.wait_ge(consts, 14)
            dve.wait_ge(scored, 1)
            V.memset(warm[:], 0.0).then_inc(misc_free, 1)
            choose(0)
            weigh(0)
            add_back(1)
            norm(1, 2)
            x_lo(1, U_X2[1])
            for ib in range(SB):
                shared_act(NBLK + ib)
            for ib in range(SB):
                act_lo(NBLK + ib)
            dve.wait_ge(scored, 2)
            V.memset(psum_w[:, 0:1], 0.0).then_inc(misc_free, 1)
            choose(1)
            weigh(1)
            rank_bank = misc[U_RANK % 2]
            dve.wait_ge(moved, U_RANK + 1)
            link(V.tensor_copy(count[:], rank_bank[:, NT * E2:(NT + 1) * E2]))
            link(V.tensor_tensor(over[:], count[:].unsqueeze(2).broadcast_to([P, E2, NT]),
                                 starts[:].unsqueeze(1).broadcast_to([P, E2, NT]), ALU.is_gt))
            link(V.tensor_reduce(tiles_of[:], over[:], AXX, ALU.add))
            link(V.tensor_tensor_scan(tiles_to[:], ones_f[:], tiles_of[:], 0.0, ALU.mult, ALU.add))
            link(V.tensor_tensor(first[:], tiles_to[:], tiles_of[:], ALU.subtract))
            link(V.tensor_scalar(first[:], first[:], float(P), None, ALU.mult))
            V.tensor_tensor(place[:], rank_bank[:, 0:NT * E2].rearrange("p (t e) -> p t e", e=E2),
                            first[:].unsqueeze(1).broadcast_to([P, NT, E2]), ALU.add).then_inc(misc_free, 1)
            dve.wait_ge(misc_free, U_RANK + 1)
            link(V.tensor_tensor(cand[:], hit[:], place[:].unsqueeze(1).broadcast_to([P, K2, NT, E2]), ALU.mult))
            link(V.tensor_reduce(spot[:], cand[:], AXX, ALU.add))
            V.tensor_copy(spot_i[:], spot[:]).then_inc(spots_ready, 1)
            link(V.tensor_tensor(past, tiles_to[0:1, :].unsqueeze(1).broadcast_to([1, 32, E2]),
                                 tile_no[:].unsqueeze(2).broadcast_to([1, 32, E2]), ALU.is_le))
            link(V.tensor_reduce(texp[:], past, AXX, ALU.add))
            V.tensor_scalar(texp_i[:], texp[:], float(E2 - 1), None, ALU.min).then_inc(texp_ready, 1)

            def add_shared(t):
                dve.wait_ge(sd_ready, t + 1)
                V.tensor_tensor(X[:, t, :], YT[t % 2][:, 0:D], X[:, t, :], ALU.add).then_inc(sd_added, 1)

            for ib in range(SB):
                shared_act(NBLK + SB + ib)
            for ib in range(SB):
                act_lo(NBLK + SB + ib)
                add_shared(ib)
            for t in range(CT, NT):
                add_shared(t)

            def slot_act(base, k):
                n = base + k
                dve.wait_ge(r_ready, n + 1)
                if not (isinstance(base, int) and n < 2):
                    dve.wait_ge(at_ready, n - 1)
                V.scalar_tensor_tensor(out=A[:, k % 2, :], in0=R[:, k % 2, :], scalar=XS[:, k % NXS, D:D + 1],
                                       in1=R[:, k % 2, :], op0=ALU.mult, op1=ALU.mult).then_inc(a_ready, 1)
                if not (isinstance(base, int) and n < NXS):
                    dve.wait_ge(y_out[k % NXS], NXS * n - NXS * (k % NXS))
                V.tensor_copy(dest[:, k % NXS:k % NXS + 1], XSd[k % NXS]).then_inc(dest_ready, 1)

            def slot_save_at(base, k):
                n = base + k
                dve.wait_ge(at_ready, n + 1)
                if not (isinstance(base, int) and n < 2):
                    dve.wait_ge(down_ready, n - 1)
                V.tensor_copy(AT[:, k % 2, :], H[2 + k % 2][:, 0:P]).then_inc(at_saved, 1)

            slot_act(0, 0)
            for n in range(1, FIRST):
                slot_save_at(0, n - 1)
                slot_act(0, n)
            with dve.Fori(0, MAIN) as i:
                for k in range(FIRST, FIRST + NXS):
                    slot_save_at(NXS * i, k - 1)
                    slot_act(NXS * i, k)
            slot_save_at(0, SLOT_TILES - 1)
            for q in range(4):
                tw = slice(2 * q, 2 * q + 2)
                dve.wait_ge(back_in[q], 16)
                link(V.tensor_tensor(X[:, tw, :], X[:, tw, :], back[:, tw, 0:D], ALU.add))
                V.tensor_tensor(X[:, tw, :], X[:, tw, :], back[:, tw, D:2 * D], ALU.add).then_inc(out_ready, 1)


_INS = ["x", "itok_BxS_13_99985", "ctx_2048", "L0_ffn_router_weight", "L0_ffn_e_bias", "L0_ffn_w_up",
        "L0_ffn_w_down", "L0_ffn_shared_up", "L0_ffn_shared_down"]


def kernel(**inputs):
    import numpy as _np
    import concourse.bacc as _bacc
    from concourse import mybir as _mybir
    from concourse.bass_utils import run_bass_kernel_spmd as _run

    nc = _bacc.Bacc("TRN2", target_bir_lowering=False, num_devices=1)
    arrays, args = {}, []
    for name in _INS:
        a = _np.ascontiguousarray(inputs[name])
        arrays[f"in_{name}"] = a
        args.append(nc.dram_tensor(f"in_{name}", a.shape, _mybir.dt.from_np(a.dtype), kind="ExternalInput").ap())
    args.append(nc.dram_tensor("out_0", (4, 256, 256), _mybir.dt.float32, kind="ExternalOutput").ap())
    build(nc, *args)
    r = _run(nc, [arrays], core_ids=[0])
    return r.results[0]["out_0"]
```

```python
import concourse.bass as bass
from concourse import mybir
from contextlib import ExitStack

F32, F32R, BF16, I32 = mybir.dt.float32, mybir.dt.float32r, mybir.dt.bfloat16, mybir.dt.int32
ALU, ACT = mybir.AluOpType, mybir.ActivationFunctionType
AXX = mybir.AxisListType.X

P = 128
TOKENS, D = 1024, 256
KB = D // P
NT = TOKENS // P
CHUNKS, CT = 2, 4
CW = CT * P
E1, F1, VOCAB = 4, 256, 12500
PER_EXPERT = VOCAB // E1
E2, F2, K2 = 16, 128, 2
GROUPS, GE = 4, 4
SH = 512
SB = SH // P
EPS = 1e-5
ROW = D + 2
SLOT_TILES = (K2 * TOKENS - E2) // P + E2
OUT_OF_BOUNDS = 4096
CONSTS = 15
NXS = 4
STEPS = CHUNKS * E1
NBLK = 2 * STEPS
NG = 8
FIRST = 7
MAIN = 5
AFTER = FIRST + MAIN * NXS


def build(nc, x, token_ids, ctx_w, router_w, e_bias, w_up, w_down, shared_up, shared_down, out):
    ctx = ExitStack()
    with ctx:
        def sb(name, shape, dt=F32):
            return ctx.enter_context(nc.sbuf_tensor(name, shape, dt))

        def sem(name):
            return ctx.enter_context(nc.semaphore(name))

        slots = nc.dram_tensor("slots", [SLOT_TILES * P, ROW], F32, kind="Internal").ap()
        routed = nc.dram_tensor("routed", [K2 * TOKENS, D], F32, kind="Internal").ap()

        X = sb("X", [P, NT, D])
        rows = sb("rows", [P, NT * K2 * ROW])
        rows_v = rows[:, :].rearrange("p (t k r) -> p t k r", t=NT, k=K2)
        back = rows[:, 0:NT * K2 * D].rearrange("p (t r) -> p t r", t=NT)
        XThi = sb("XThi", [P, KB, TOKENS], F32R)
        XTlo = sb("XTlo", [P, KB, TOKENS], F32R)
        ctx_raw = sb("ctx_raw", [P, E1 * KB, D])
        WThi = sb("WThi", [P, E1, KB, F1], F32R)
        WTlo = sb("WTlo", [P, E1, KB, F1], F32R)
        rw_raw = sb("rw_raw", [P, D])
        RWhi = sb("RWhi", [P, KB, P], F32R)
        RWlo = sb("RWlo", [P, KB, P], F32R)
        bias = sb("bias", [P, E2])
        su_raw = sb("su_raw", [P, KB, SH])
        SUhi = sb("SUhi", [P, KB, SH], F32R)
        SUlo = sb("SUlo", [P, KB, SH], F32R)
        sd_raw = sb("sd_raw", [P, SB, D])
        SDhi = sb("SDhi", [P, SB, D], F32R)
        SDlo = sb("SDlo", [P, SB, D], F32R)
        WU = sb("WU", [P, E2 * KB * F2])
        WD = sb("WD", [P, E2 * D])
        ids = sb("ids", [P, TOKENS], I32)
        code = sb("code", [P, TOKENS], BF16)
        sg = sb("sg", [P, 4, CW])
        sq = sb("sq", [P, 2, CW])
        act1 = sb("act1", [P, 4, CW])
        Ghi = sb("Ghi", [P, NG, CW], F32R)
        Glo = sb("Glo", [P, NG, CW], F32R)
        yTs = sb("yTs", [P, KB, CW])
        logits_T = yTs[0:E2, 0, :]
        stats = sb("stats", [P, NT, 6])
        mv = sb("mv", [P, NT, 2])
        rstd = sb("rstd", [P, NT])
        shift = sb("shift", [P, NT])
        var = sb("var", [P, NT])
        minus_half_var = sb("minus_half_var", [P, NT])
        guess = sb("guess", [P, NT], I32)
        XS = sb("XS", [P, NXS, ROW])
        meta = sb("meta", [P, SLOT_TILES * 2], I32)
        XST = sb("XST", [P, 2, D])
        R = sb("R", [P, 2, F2])
        A = sb("A", [P, 2, F2])
        AT = sb("AT", [P, 2, P])
        Y = ctx_raw[:, 0:NXS, :]
        dest = sb("dest", [P, NXS], I32)
        ident = sb("ident", [P, P])
        before = sb("before", [P, P], BF16)
        ones = sb("ones", [P, P], BF16)
        lower_group = sb("lower_group", [P, GROUPS, GROUPS])
        expert_no = sb("expert_no", [P, E2])
        starts = sb("starts", [P, NT])
        tile_no = sb("tile_no", [1, 32])
        pad_row = sb("pad_row", [P, ROW])
        ones_f = sb("ones_f", [P, E2])
        SC = sb("SC", [P, NT, E2])
        biased = sb("biased", [P, NT, E2])
        pairs = sb("pairs", [P, NT * GROUPS, 6])
        gscore = sb("gscore", [P, NT, GROUPS])
        beats = sb("beats", [P, NT, GROUPS, GROUPS])
        ties = sb("ties", [P, NT, GROUPS, GROUPS])
        grank = sb("grank", [P, NT, GROUPS])
        masked = sb("masked", [P, NT, E2])
        top = sb("top", [P, NT, 8])
        top_i = sb("top_i", [P, NT, 8], mybir.dt.uint32)
        cand = sb("cand", [P, K2, NT, E2])
        hit = sb("hit", [P, K2, NT, E2])
        chosen = sb("chosen", [P, NT, E2], BF16)
        pv = sb("pv", [P, K2, NT])
        psum_w = sb("psum_w", [P, NT])
        count = sb("count", [P, E2])
        over = sb("over", [P, E2, NT])
        tiles_of = sb("tiles_of", [P, E2])
        tiles_to = sb("tiles_to", [P, E2])
        first = sb("first", [P, E2])
        place = sb("place", [P, NT, E2])
        spot = sb("spot", [P, K2, NT])
        spot_i = sb("spot_i", [P, K2, NT], I32)
        past = yTs[0:1, 0, :].rearrange("p (n e) -> p n e", e=E2)
        texp = sb("texp", [1, 32])
        texp_i = sb("texp_i", [1, 32], I32)

        misc = [ctx.enter_context(nc.psum_tensor(f"misc{i}", [P, CW], F32)) for i in range(2)]
        H = [ctx.enter_context(nc.psum_tensor(f"H{i}", [P, CW], F32)) for i in range(4)]
        YT = [ctx.enter_context(nc.psum_tensor(f"YT{i}", [P, CW], F32)) for i in range(2)]

        W_BANKS = [H[2], H[3], YT[0], YT[1]]

        x_in = [sem(f"x_in{c}") for c in range(CHUNKS)]
        ids_in, ctx_in, rw_in, bias_in = sem("ids_in"), sem("ctx_in"), sem("rw_in"), sem("bias_in")
        su_in, sd_in, wu_in, wd_in = sem("su_in"), sem("sd_in"), sem("wu_in"), sem("wd_in")
        pads_out = sem("pads_out")
        consts = sem("consts")
        dve_chain = sem("dve_chain")
        normed = sem("normed")
        moved = sem("moved")
        hi_done = sem("hi_done")
        misc_free = sem("misc_free")
        w_moved = sem("w_moved")
        whi_done = sem("whi_done")
        wlo_done = sem("wlo_done")
        shi_done = sem("shi_done")
        slo_done = sem("slo_done")
        stats_ready = sem("stats_ready")
        copied = sem("copied")
        logits_saved = sem("logits_saved")
        h_ready = sem("h_ready")
        sq_done = sem("sq_done")
        act_ready = sem("act_ready")
        ghi_done, glo_done = sem("ghi_done"), sem("glo_done")
        y_done = sem("y_done")
        yT_saved = sem("yT_saved")
        scored = sem("scored")
        chosen_ready = sem("chosen_ready")
        spots_ready = sem("spots_ready")
        texp_ready = sem("texp_ready")
        sd_ready = sem("sd_ready")
        sd_added = sem("sd_added")
        rows_out = sem("rows_out")
        xs_in = [sem(f"xs_in{b}") for b in range(NXS)]
        y_out = [sem(f"y_out{b}") for b in range(NXS)]
        xt_ready, xt_saved = sem("xt_ready"), sem("xt_saved")
        up_ready, r_ready, a_ready = sem("up_ready"), sem("r_ready"), sem("a_ready")
        at_ready, at_saved = sem("at_ready"), sem("at_saved")
        down_ready, y_saved = sem("down_ready"), sem("y_saved")
        meta_ready, dest_ready = sem("meta_ready"), sem("dest_ready")
        scatters_begun = sem("scatters_begun")
        back_in = [sem(f"back_in{c}") for c in range(4)]
        out_ready = sem("out_ready")
        out_done = sem("out_done")

        U_X = [[0, 1], [2, 3]]
        U_RW = 4
        U_BACK = [[5, 6], [11, 12]]
        U_X2 = [[7, 8], [13, 14]]
        U_LOGITS = [[9, 10], [15, 16]]
        U_RANK = 17
        SPLITS = [0, 1, 2, 3, 4, 7, 8, 13, 14]

        x_t = x.rearrange("b (s p) d -> p (b s) d", p=P)
        out_t = out.rearrange("b (s p) d -> p (b s) d", p=P)
        routed_t = routed.rearrange("(t p k) d -> p t (k d)", p=P, k=K2)
        slots_t = slots.rearrange("(n p) r -> n p r", p=P)

        block = ctx.enter_context(nc.Block())

        @block.sync
        def _(sp):
            for c in range(CHUNKS):
                sp.dma_start(X[:, c * CT:(c + 1) * CT, :], x_t[:, c * CT:(c + 1) * CT, :]).then_inc(x_in[c], 16)
            sp.dma_start(su_raw[:], shared_up.rearrange("(k p) n -> p k n", p=P)).then_inc(su_in, 16)
            sp.dma_start(sd_raw[:], shared_down.rearrange("(k p) n -> p k n", p=P)).then_inc(sd_in, 16)
            sp.dma_start(WU[:].rearrange("p (e k f) -> p e k f", e=E2, k=KB),
                         w_up.rearrange("e (k p) f -> p e k f", p=P)).then_inc(wu_in, 16)
            sp.dma_start(WD[:].rearrange("p (e d) -> p e d", e=E2),
                         w_down.rearrange("e p d -> p e d")).then_inc(wd_in, 16)
            sp.wait_ge(rows_out, 16 * K2 * NT)

            def load(n, rows_of, b):
                if not (isinstance(n, int) and n < NXS):
                    sp.wait_ge(xt_ready, n - NXS + 1)
                    sp.wait_ge(meta_ready, n - NXS + 1)
                sp.dma_start(XS[:, b, :], rows_of).then_inc(xs_in[b], 16)

            for n in range(NXS):
                load(n, slots_t[n], n)
            with sp.Fori(1, SLOT_TILES // NXS) as i:
                for b in range(NXS):
                    load(NXS * i + b, slots[bass.ds(NXS * P * i + b * P, P), :], b)
            for n in range(SLOT_TILES // NXS * NXS, SLOT_TILES):
                load(n, slots_t[n], n % NXS)
            for b in range(NXS):
                sp.wait_ge(y_out[b], 16 * ((SLOT_TILES - 1 - b) // NXS + 1))
            for q in range(4):
                sp.dma_start(back[:, 2 * q:2 * q + 2, :], routed_t[:, 2 * q:2 * q + 2, :]).then_inc(back_in[q], 16)
            for q in range(4):
                sp.wait_ge(out_ready, q + 1)
                sp.dma_start(out_t[:, 2 * q:2 * q + 2, :], X[:, 2 * q:2 * q + 2, :]).then_inc(out_done, 16)
            sp.wait_ge(out_done, 16 * 4)
            sp.wait_ge(pads_out, 16)

        @block.gpsimd
        def _(pool):
            n = [0]

            def const(ins):
                n[0] += 1
                ins.then_inc(consts, 1)

            const(pool.memset(rw_raw[:], 0.0))
            const(pool.memset(ident[:], 0.0))
            const(pool.memset(before[:], 1.0))
            const(pool.memset(lower_group[:], 1.0))
            const(pool.memset(pad_row[:], 0.0))
            const(pool.memset(ones[:], 1.0))
            const(pool.memset(ones_f[:], 1.0))
            pool.wait_ge(consts, n[0])
            const(pool.affine_select(out=ident[:], in_=ident[:], compare_op=ALU.not_equal, fill=1.0, base=0,
                                     pattern=[[-1, P]], channel_multiplier=1))
            const(pool.affine_select(out=before[:], in_=before[:], compare_op=ALU.is_gt, fill=0.0, base=0,
                                     pattern=[[1, P]], channel_multiplier=-1))
            const(pool.affine_select(out=lower_group[:], in_=lower_group[:], compare_op=ALU.is_gt, fill=0.0,
                                     base=0, pattern=[[1, GROUPS], [-1, GROUPS]], channel_multiplier=0))
            const(pool.memset(pad_row[:, D + 1:D + 2].bitcast(I32), OUT_OF_BOUNDS))
            const(pool.iota(expert_no[:], pattern=[[1, E2]], base=0, channel_multiplier=0,
                            allow_small_or_imprecise_dtypes=True))
            const(pool.iota(starts[:], pattern=[[P, NT]], base=0, channel_multiplier=0,
                            allow_small_or_imprecise_dtypes=True))
            const(pool.iota(tile_no[:], pattern=[[1, 32]], base=0, channel_multiplier=0,
                            allow_small_or_imprecise_dtypes=True))
            const(pool.iota(rows_v[:, :, :, D + 1:D + 2].bitcast(I32),
                            pattern=[[K2 * P, NT], [1, K2], [0, 1]], base=0, channel_multiplier=K2))
            assert n[0] == CONSTS
            for k, (raw, hi, lo, landed) in enumerate(((su_raw, SUhi, SUlo, su_in), (sd_raw, SDhi, SDlo, sd_in))):
                pool.wait_ge(landed, 16)
                pool.tensor_copy(hi[:], raw[:]).then_inc(shi_done, 1)
                pool.wait_ge(shi_done, k + 1)
                pool.tensor_tensor(lo[:], raw[:], hi[:].bitcast(F32), ALU.subtract).then_inc(slo_done, 1)
            pool.wait_ge(consts, CONSTS)
            pool.wait_ge(wu_in, 16)
            pool.wait_ge(wd_in, 16)
            pool.dma_start(slots.rearrange("(n p) r -> p n r", p=P),
                           pad_row[:].unsqueeze(1).broadcast_to([P, SLOT_TILES, ROW])).then_inc(pads_out, 16)
            for t in range(NT):
                pool.wait_ge(normed, NT + t + 1)
                pool.tensor_copy(rows_v[:, t, 1, 0:D], rows_v[:, t, 0, 0:D]).then_inc(copied, 1)
            pool.wait_ge(pads_out, 16)
            pool.wait_ge(spots_ready, 1)
            pool.wait_ge(copied, NT)
            for t in range(NT):
                for k in range(K2):
                    pool.indirect_dma_start(
                        slots, bass.IndirectOffsetOnAxis(ap=spot_i[:, k, t:t + 1], axis=0),
                        rows_v[:, t, k, :], None, bounds_check=SLOT_TILES * P - 1,
                        oob_is_err=False).then_inc(rows_out, 16)

            def scatter(b, n):
                pool.wait_ge(y_saved, n + 1)
                pool.wait_ge(dest_ready, n + 1)
                pool.sem_inc(scatters_begun, 1)
                pool.indirect_dma_start(
                    routed, bass.IndirectOffsetOnAxis(ap=dest[:, b:b + 1], axis=0),
                    Y[:, b, :], None, bounds_check=K2 * TOKENS - 1, oob_is_err=False).then_inc(y_out[b], 16)

            with pool.Fori(0, SLOT_TILES // NXS) as i:
                for b in range(NXS):
                    scatter(b, NXS * i + b)
            for n_ in range(SLOT_TILES // NXS * NXS, SLOT_TILES):
                scatter(n_ % NXS, n_)

        @block.tensor
        def _(pe):
            def use(u):
                if u >= 2:
                    pe.wait_ge(misc_free, u - 1)
                return misc[u % 2]

            def transpose_x(c, kb, u, reader_sem, value):
                bank = use(u)
                pe.wait_ge(reader_sem, value)
                for j in range(CT):
                    last = pe.transpose(bank[:, j * P:(j + 1) * P],
                                        rows_v[:, c * CT + j, 0, kb * P:(kb + 1) * P], ident[:])
                last.then_inc(moved, 1)

            def transpose_w(e):
                for kb in range(KB):
                    for ib in range(KB):
                        last = pe.transpose(W_BANKS[e][:, kb * F1 + ib * P:kb * F1 + (ib + 1) * P],
                                            ctx_raw[:, e * KB + ib, kb * P:(kb + 1) * P], ident[:])
                last.then_inc(w_moved, 1)

            def split_product(dst, pairs_of, sg_check=False):
                terms = [t for (ahi, alo, bhi, blo) in pairs_of for t in ((ahi, bhi), (ahi, blo), (alo, bhi))]
                for j, (a, b) in enumerate(terms):
                    last = pe.matmul(dst, a, b, start=(j == 0), stop=(j == len(terms) - 1))
                return last

            def hidden(s):
                c, e = divmod(s, E1)
                if e == 0:
                    for kb in range(KB):
                        u = SPLITS.index(U_X[c][kb]) + 1
                        pe.wait_ge(hi_done, u)
                        pe.wait_ge(misc_free, U_X[c][kb] + 1)
                pe.wait_ge(whi_done, e + 1)
                pe.wait_ge(wlo_done, e + 1)
                for b in range(2):
                    n = 2 * s + b
                    if n >= 4:
                        pe.wait_ge(sq_done, n - 3)
                    w = slice(b * P, (b + 1) * P)
                    cw = slice(c * CW, (c + 1) * CW)
                    split_product(H[n % 4][:], [(WThi[:, e, kb, w], WTlo[:, e, kb, w],
                                                 XThi[:, kb, cw], XTlo[:, kb, cw]) for kb in range(KB)]
                                  ).then_inc(h_ready, 1)

            def project(s):
                c, e = divmod(s, E1)
                if e == 0:
                    if c:
                        pe.wait_ge(yT_saved, 2 * c)
                    else:
                        pe.wait_ge(wlo_done, E1)
                for b in range(2):
                    n = 2 * s + b
                    pe.wait_ge(ghi_done, n + 1)
                    pe.wait_ge(glo_done, n + 1)
                    for db in range(KB):
                        w = slice(db * P, (db + 1) * P)
                        g = n % NG
                        terms = ((WThi, Ghi), (WThi, Glo), (WTlo, Ghi))
                        for j, (a, gg) in enumerate(terms):
                            last = pe.matmul(YT[db][:], a[:, e, b, w], gg[:, g, :],
                                             start=(e == 0 and b == 0 and j == 0),
                                             stop=(e == E1 - 1 and b == 1 and j == 2))
                last.then_inc(y_done, 1)

            def transpose_back(c):
                for half in range(2):
                    bank = use(U_BACK[c][half])
                    pe.wait_ge(yT_saved, 2 * c + 2)
                    for j in range(2):
                        for db in range(KB):
                            t = 2 * half + j
                            last = pe.transpose(bank[:, j * D + db * P:j * D + (db + 1) * P],
                                                yTs[:, db, t * P:(t + 1) * P], ident[:])
                    last.then_inc(moved, 1)

            def route(c):
                bank = use(U_LOGITS[c][0])
                for u in (U_X2[c][1], U_RW):
                    pe.wait_ge(hi_done, SPLITS.index(u) + 1)
                    pe.wait_ge(misc_free, u + 1)
                cw = slice(c * CW, (c + 1) * CW)
                split_product(bank[:], [(RWhi[:, kb, :], RWlo[:, kb, :], XThi[:, kb, cw], XTlo[:, kb, cw])
                                        for kb in range(KB)]).then_inc(moved, 1)

            def route_back(c):
                bank = use(U_LOGITS[c][1])
                pe.wait_ge(logits_saved, c + 1)
                for j in range(CT):
                    last = pe.transpose(bank[:, j * E2:(j + 1) * E2], logits_T[:, j * P:(j + 1) * P],
                                        ident[0:E2, 0:E2])
                last.then_inc(moved, 1)

            def shared_up_blocks(c, blocks):
                for ib in blocks:
                    n = NBLK + SB * c + ib
                    pe.wait_ge(slo_done, 1)
                    pe.wait_ge(sq_done, n - 3)
                    w = slice(ib * P, (ib + 1) * P)
                    cw = slice(c * CW, (c + 1) * CW)
                    split_product(H[n % 4][:], [(SUhi[:, kb, w], SUlo[:, kb, w],
                                                 XThi[:, kb, cw], XTlo[:, kb, cw]) for kb in range(KB)]
                                  ).then_inc(h_ready, 1)

            def shared_down_tiles(c):
                pe.wait_ge(slo_done, 2)
                pe.wait_ge(yT_saved, 2 * CHUNKS)
                pe.wait_ge(ghi_done, NBLK + SB * (c + 1))
                pe.wait_ge(glo_done, NBLK + SB * (c + 1))
                for j in range(CT):
                    t = c * CT + j
                    if t >= 2:
                        pe.wait_ge(sd_added, t - 1)
                    tw = slice(j * P, (j + 1) * P)
                    g = [(NBLK + SB * c + ib) % NG for ib in range(SB)]
                    split_product(YT[t % 2][:, 0:D], [(Ghi[:, g[ib], tw], Glo[:, g[ib], tw],
                                                       SDhi[:, ib, :], SDlo[:, ib, :]) for ib in range(SB)]
                                  ).then_inc(sd_ready, 1)

            pe.wait_ge(consts, CONSTS)
            pe.wait_ge(ctx_in, 16)
            for e in range(E1):
                transpose_w(e)
            for kb in range(KB):
                transpose_x(0, kb, U_X[0][kb], normed, CT)
            hidden(0)
            for kb in range(KB):
                transpose_x(1, kb, U_X[1][kb], normed, 2 * CT)
            hidden(1)
            project(0)
            hidden(2)
            project(1)
            bank = use(U_RW)
            pe.wait_ge(rw_in, 16)
            for kb in range(KB):
                last = pe.transpose(bank[:, kb * P:(kb + 1) * P], rw_raw[:, kb * P:(kb + 1) * P], ident[:])
            last.then_inc(moved, 1)
            hidden(3)
            project(2)
            hidden(4)
            project(3)
            hidden(5)
            transpose_back(0)
            project(4)
            hidden(6)
            for kb in range(KB):
                transpose_x(0, kb, U_X2[0][kb], normed, 3 * CT)
            project(5)
            hidden(7)
            route(0)
            project(6)
            route_back(0)
            project(7)
            shared_up_blocks(0, (0, 1))
            transpose_back(1)
            shared_up_blocks(0, (2, 3))
            for kb in range(KB):
                transpose_x(1, kb, U_X2[1][kb], normed, 4 * CT)
            route(1)
            shared_up_blocks(1, (0,))
            route_back(1)
            shared_up_blocks(1, (1, 2))
            bank = use(U_RANK)
            pe.wait_ge(chosen_ready, CHUNKS)
            ranks = bank[:, 0:NT * E2]
            pe.matmul(ranks, before[:], chosen[:].rearrange("p t e -> p (t e)"), start=True, stop=False)
            for t in range(NT - 1):
                pe.matmul(bank[:, (t + 1) * E2:NT * E2].rearrange("p (t e) -> p t e", e=E2), ones[:],
                          chosen[:, t:t + 1, :].broadcast_to([P, NT - 1 - t, E2]),
                          start=False, stop=(t == NT - 2))
            for t in range(NT):
                last = pe.matmul(bank[:, NT * E2:(NT + 1) * E2], ones[:], chosen[:, t, :],
                                 start=(t == 0), stop=(t == NT - 1))
            last.then_inc(moved, 1)
            shared_up_blocks(1, (3,))
            shared_down_tiles(0)
            shared_down_tiles(1)

            def slot_transpose(base, k):
                n = base + k
                pe.wait_ge(xs_in[k % NXS], NXS * n + (16 - NXS * (k % NXS)))
                if not (isinstance(base, int) and n < 2):
                    pe.wait_ge(xt_saved, n - 1)
                for kb in range(KB):
                    last = pe.transpose(misc[k % 2][:, kb * P:(kb + 1) * P],
                                        XS[:, k % NXS, kb * P:(kb + 1) * P], ident[:])
                last.then_inc(xt_ready, 1)

            def experts(n, count):
                return nc.values_load_multi_w_load_instructions(
                    texp_i[0:1, bass.ds(n, count)], engines=[mybir.EngineType.PE], min_val=0, max_val=E2 - 1,
                    skip_runtime_bounds_check_because="a count of experts, clamped to E2 - 1 where it is made")[1]

            def slot_up(base, k, e):
                n = base + k
                pe.wait_ge(xt_saved, n + 1)
                if not (isinstance(base, int) and n < 2):
                    pe.wait_ge(r_ready, n - 1)
                for kb in range(KB):
                    last = pe.matmul(H[k % 2][:, 0:F2], XST[:, k % 2, kb * P:(kb + 1) * P],
                                     WU[:, bass.ds(e * (KB * F2) + kb * F2, F2)],
                                     start=(kb == 0), stop=(kb == KB - 1))
                last.then_inc(up_ready, 1)

            def slot_act_transpose(base, k):
                n = base + k
                pe.wait_ge(a_ready, n + 1)
                if not (isinstance(base, int) and n < 2):
                    pe.wait_ge(at_saved, n - 1)
                pe.transpose(H[2 + k % 2][:, 0:P], A[:, k % 2, :], ident[:]).then_inc(at_ready, 1)

            def slot_down(base, k, e):
                n = base + k
                pe.wait_ge(at_saved, n + 1)
                if not (isinstance(base, int) and n < 2):
                    pe.wait_ge(y_saved, n - 1)
                pe.matmul(YT[k % 2][:, 0:D], AT[:, k % 2, :], WD[:, bass.ds(e * D, D)],
                          start=True, stop=True).then_inc(down_ready, 1)

            pe.wait_ge(misc_free, U_RANK + 1)
            pe.wait_ge(sd_added, NT)
            pe.wait_ge(sq_done, NBLK + CHUNKS * SB)
            pe.wait_ge(wu_in, 16)
            pe.wait_ge(wd_in, 16)
            pe.wait_ge(texp_ready, 1)
            def slot_step(base, k, e_this, e_down):
                if isinstance(base, int) and base + k >= SLOT_TILES:
                    e_this = None
                if e_this is not None:
                    slot_up(base, k, e_this)
                if not (isinstance(base, int) and not 0 <= base + k - 1 < SLOT_TILES):
                    slot_act_transpose(base, k - 1)
                if e_down is not None:
                    slot_down(base, k - 2, e_down)
                if not (isinstance(base, int) and base + k + 2 >= SLOT_TILES):
                    slot_transpose(base, k + 2)

            slot_transpose(0, 0)
            slot_transpose(0, 1)
            e = experts(0, FIRST)
            for n in range(FIRST):
                slot_step(0, n, e[n], e[n - 2] if n >= 2 else None)
            with pe.Fori(0, MAIN) as i:
                e = experts(NXS * i + (FIRST - 2), NXS + 2)
                for j in range(NXS):
                    slot_step(NXS * i, FIRST + j, e[j + 2], e[j])
            e = experts(AFTER - 2, SLOT_TILES - AFTER + 2)
            for n in range(AFTER, SLOT_TILES + 2):
                j = n - AFTER
                slot_step(0, n, e[j + 2] if n < SLOT_TILES else None, e[j])

        @block.scalar
        def _(act):
            act.dma_start(ctx_raw[:], ctx_w.rearrange("e (b p) d -> p (e b) d", p=P)).then_inc(ctx_in, 16)
            act.dma_start(ids[:], token_ids.rearrange("(o b) s -> o (b s)", o=1).broadcast_to([P, TOKENS])
                          ).then_inc(ids_in, 16)
            act.wait_ge(consts, 1)
            act.dma_start(rw_raw[0:E2, :], router_w).then_inc(rw_in, 16)
            act.dma_start(bias[:], e_bias.rearrange("(o e) -> o e", o=1).broadcast_to([P, E2])
                          ).then_inc(bias_in, 16)

            def split_hi(u, dst):
                act.wait_ge(moved, u + 1)
                src = misc[u % 2][:]
                if len(dst.shape) == 3:
                    src = misc[u % 2][:, 0:dst.shape[1] * dst.shape[2]].rearrange("p (k n) -> p k n", k=dst.shape[1])
                nc.scalar.activation(dst, src, ACT.Copy).then_inc(hi_done, 1)

            def x_hi(c, uses):
                for kb in range(KB):
                    split_hi(uses[kb], XThi[:, kb, c * CW:(c + 1) * CW])

            def take(n, func):
                act.wait_ge(h_ready, n + 1)
                if n >= 4:
                    act.wait_ge(act_ready, n - 3)
                i = nc.scalar.activation(sg[:, n % 4, :], H[n % 4][:], func)
                if func == ACT.Relu:
                    i.then_inc(sq_done, 1)
                    return
                if n >= 2:
                    act.wait_ge(act_ready, n - 1)
                nc.scalar.activation(sq[:, n % 2, :], H[n % 4][:], ACT.Square).then_inc(sq_done, 1)

            def act_hi(n):
                act.wait_ge(act_ready, n + 1)
                if n >= NG:
                    act.wait_ge(y_done, (n - NG) // 2 + 1)
                nc.scalar.activation(Ghi[:, n % NG, :], act1[:, n % 4, :], ACT.Copy).then_inc(ghi_done, 1)

            def step(s):
                for b in range(2):
                    take(2 * s + b, ACT.Sigmoid)
                for b in range(2):
                    act_hi(2 * s + b)

            def save_y(c):
                act.wait_ge(y_done, E1 * (c + 1))
                if c:
                    act.wait_ge(moved, U_BACK[c - 1][1] + 1)
                for db in range(KB):
                    nc.scalar.activation(yTs[:, db, :], YT[db][:], ACT.Copy).then_inc(yT_saved, 1)

            def apply_norm(call):
                c = call % CHUNKS
                act.wait_ge(stats_ready, call + 1)
                for t in range(c * CT, (c + 1) * CT):
                    nc.scalar.activation(rows_v[:, t, 0, 0:D], X[:, t, :], ACT.Identity, bias=shift[:, t:t + 1],
                                         scale=rstd[:, t:t + 1]).then_inc(normed, 1)

            def w_hi(e):
                act.wait_ge(w_moved, e + 1)
                nc.scalar.activation(WThi[:, e], W_BANKS[e][:].rearrange("p (k n) -> p k n", k=KB),
                                     ACT.Copy).then_inc(whi_done, 1)

            def scores(c):
                act.wait_ge(moved, U_LOGITS[c][1] + 1)
                nc.scalar.activation(SC[:, c * CT:(c + 1) * CT, :],
                                     misc[U_LOGITS[c][1] % 2][:, 0:CT * E2].rearrange("p (t e) -> p t e", e=E2),
                                     ACT.Sigmoid).then_inc(scored, 1)

            w_hi(0)
            w_hi(1)
            apply_norm(0)
            x_hi(0, U_X[0])
            w_hi(2)
            w_hi(3)
            for b in range(2):
                take(b, ACT.Sigmoid)
            apply_norm(1)
            for b in range(2):
                act_hi(b)
            x_hi(1, U_X[1])
            step(1)
            step(2)
            split_hi(U_RW, RWhi[:])
            step(3)
            step(4)
            save_y(0)
            for b in range(2):
                take(2 * 5 + b, ACT.Sigmoid)
            apply_norm(2)
            for b in range(2):
                act_hi(2 * 5 + b)
            x_hi(0, U_X2[0])
            step(6)
            step(7)
            scores(0)
            save_y(1)
            for ib in range(SB):
                take(NBLK + ib, ACT.Relu)
            apply_norm(3)
            x_hi(1, U_X2[1])
            scores(1)
            for ib in range(SB):
                act_hi(NBLK + ib)
            for ib in range(SB):
                take(NBLK + SB + ib, ACT.Relu)
            for ib in range(SB):
                act_hi(NBLK + SB + ib)

            def slot_save_x(base, k):
                n = base + k
                act.wait_ge(xt_ready, n + 1)
                if not (isinstance(base, int) and n < 2):
                    act.wait_ge(up_ready, n - 1)
                nc.scalar.activation(XST[:, k % 2, :], misc[k % 2][:, 0:D], ACT.Copy).then_inc(xt_saved, 1)

            def slot_relu(base, k):
                n = base + k
                act.wait_ge(up_ready, n + 1)
                if not (isinstance(base, int) and n < 2):
                    act.wait_ge(a_ready, n - 1)
                nc.scalar.activation(R[:, k % 2, :], H[k % 2][:, 0:F2], ACT.Relu).then_inc(r_ready, 1)

            def slot_save_y(base, k):
                n = base + k
                act.wait_ge(down_ready, n + 1)
                if not (isinstance(base, int) and n < NXS):
                    act.wait_ge(y_out[k % NXS], NXS * n - NXS * (k % NXS))
                nc.scalar.activation(Y[:, k % NXS, :], YT[k % 2][:, 0:D], ACT.Copy).then_inc(y_saved, 1)

            def slot_step(base, k):
                at = (lambda m: 0 <= base + m < SLOT_TILES) if isinstance(base, int) else (lambda m: True)
                if at(k):
                    slot_relu(base, k)
                if at(k - 2):
                    slot_save_y(base, k - 2)
                if at(k + 2):
                    slot_save_x(base, k + 2)

            slot_save_x(0, 0)
            slot_save_x(0, 1)
            for n in range(FIRST):
                slot_step(0, n)
            with act.Fori(0, MAIN) as i:
                for k in range(FIRST, FIRST + NXS):
                    slot_step(NXS * i, k)
            for n in range(AFTER, SLOT_TILES + 2):
                slot_step(0, n)

        @block.vector
        def _(dve):
            chain = [0]

            def then(ins):
                chain[0] += 1
                ins.then_inc(dve_chain, 1)

            def settle():
                dve.wait_ge(dve_chain, chain[0])

            def link(ins):
                then(ins)
                settle()

            V = nc.vector

            def norm(c):
                ts_ = range(c * CT, (c + 1) * CT)
                for t in ts_:
                    then(V.bn_stats(stats[:, t, :], X[:, t, :]))
                settle()
                for t in ts_:
                    then(V.bn_aggr(mv[:, t, :], stats[:, t, :]))
                settle()
                cs = slice(c * CT, (c + 1) * CT)
                y = rstd[:, cs]
                then(V.tensor_scalar(minus_half_var[:, cs], mv[:, cs, 1], EPS, -0.5, ALU.add, ALU.mult))
                link(V.tensor_scalar(var[:, cs], mv[:, cs, 1], EPS, None, ALU.add))
                link(V.tensor_scalar(guess[:, cs], var[:, cs].bitcast(I32), 1, None, ALU.arith_shift_right))
                link(V.tensor_scalar(y.bitcast(I32), guess[:, cs], -1.0, float(0x5F3759DF), ALU.mult, ALU.add))
                for _ in range(3):
                    link(V.tensor_tensor(var[:, cs], y, y, ALU.mult))
                    link(V.tensor_tensor(var[:, cs], var[:, cs], minus_half_var[:, cs], ALU.mult))
                    link(V.scalar_tensor_tensor(out=y, in0=var[:, cs], scalar=1.5, in1=y, op0=ALU.add, op1=ALU.mult))
                V.scalar_tensor_tensor(out=shift[:, cs], in0=mv[:, cs, 0], scalar=-1.0, in1=y, op0=ALU.mult,
                                       op1=ALU.mult).then_inc(stats_ready, 1)

            def w_lo(e):
                dve.wait_ge(whi_done, e + 1)
                V.tensor_tensor(WTlo[:, e], W_BANKS[e][:].rearrange("p (k n) -> p k n", k=KB),
                                WThi[:, e].bitcast(F32), ALU.subtract).then_inc(wlo_done, 1)

            def split_lo(u, hi, lo):
                dve.wait_ge(hi_done, SPLITS.index(u) + 1)
                src = misc[u % 2][:]
                if len(hi.shape) == 3:
                    src = misc[u % 2][:, 0:hi.shape[1] * hi.shape[2]].rearrange("p (k n) -> p k n", k=hi.shape[1])
                V.tensor_tensor(lo, src, hi.bitcast(F32), ALU.subtract).then_inc(misc_free, 1)

            def x_lo(c, uses):
                for kb in range(KB):
                    cw = slice(c * CW, (c + 1) * CW)
                    split_lo(uses[kb], XThi[:, kb, cw], XTlo[:, kb, cw])

            def encode(c):
                if c == 0:
                    dve.wait_ge(ids_in, 16)
                cw = slice(c * CW, (c + 1) * CW)
                link(V.tensor_scalar(code[:, cw], ids[:, cw], float(PER_EXPERT), None, ALU.is_ge))
                for e in range(2, E1):
                    link(V.scalar_tensor_tensor(out=code[:, cw], in0=ids[:, cw], scalar=float(e * PER_EXPERT),
                                                in1=code[:, cw], op0=ALU.is_ge, op1=ALU.add))

            def act_lo(n):
                dve.wait_ge(ghi_done, n + 1)
                if n >= NG:
                    dve.wait_ge(y_done, (n - NG) // 2 + 1)
                V.tensor_tensor(Glo[:, n % NG, :], act1[:, n % 4, :], Ghi[:, n % NG, :].bitcast(F32),
                                ALU.subtract).then_inc(glo_done, 1)

            def step(s):
                c, e = divmod(s, E1)
                cw = slice(c * CW, (c + 1) * CW)
                for b in range(2):
                    n = 2 * s + b
                    dve.wait_ge(sq_done, n + 1)
                    then(V.scalar_tensor_tensor(out=sg[:, n % 4, :], in0=code[:, cw], scalar=float(e),
                                                in1=sg[:, n % 4, :], op0=ALU.is_equal, op1=ALU.mult))
                settle()
                for b in range(2):
                    n = 2 * s + b
                    if n >= 4:
                        dve.wait_ge(ghi_done, n - 3)
                        dve.wait_ge(glo_done, n - 3)
                    V.tensor_tensor(act1[:, n % 4, :], sg[:, n % 4, :], sq[:, n % 2, :],
                                    ALU.mult).then_inc(act_ready, 1)
                for b in range(2):
                    act_lo(2 * s + b)

            def shared_act(n):
                dve.wait_ge(sq_done, n + 1)
                dve.wait_ge(ghi_done, n - 3)
                dve.wait_ge(glo_done, n - 3)
                V.tensor_tensor(act1[:, n % 4, :], sg[:, n % 4, :], sg[:, n % 4, :], ALU.mult).then_inc(act_ready, 1)

            def add_back(c):
                for half in range(2):
                    u = U_BACK[c][half]
                    t = c * CT + 2 * half
                    dve.wait_ge(moved, u + 1)
                    V.tensor_tensor(X[:, t:t + 2, :].rearrange("p t d -> p (t d)"), misc[u % 2][:],
                                    X[:, t:t + 2, :].rearrange("p t d -> p (t d)"), ALU.add).then_inc(misc_free, 1)
                dve.wait_ge(misc_free, U_BACK[c][1] + 1)

            def save_logits(c):
                u = U_LOGITS[c][0]
                dve.wait_ge(moved, u + 1)
                V.tensor_copy(logits_T, misc[u % 2][0:E2, :]).then_inc(misc_free, 1)
                dve.wait_ge(misc_free, u + 1)
                dve.sem_inc(logits_saved, 1)

            def score_groups(c):
                tw = slice(c * CT, (c + 1) * CT)
                gw = slice(c * CT * GROUPS, (c + 1) * CT * GROUPS)
                dve.wait_ge(scored, c + 1)
                V.tensor_tensor(biased[:, tw, :], SC[:, tw, :], bias[:].unsqueeze(1).broadcast_to([P, CT, E2]),
                                ALU.add).then_inc(misc_free, 1)
                dve.wait_ge(misc_free, U_LOGITS[c][1] + 1)
                s4 = biased[:, tw, :].rearrange("p t (g e) -> p (t g) e", g=GROUPS)
                then(V.tensor_tensor(pairs[:, gw, 0:3], s4[:, :, 0:3], s4[:, :, 1:4], ALU.add))
                then(V.tensor_tensor(pairs[:, gw, 3:5], s4[:, :, 0:2], s4[:, :, 2:4], ALU.add))
                link(V.tensor_tensor(pairs[:, gw, 5:6], s4[:, :, 0:1], s4[:, :, 3:4], ALU.add))
                gs = gscore[:, tw, :]
                then(V.tensor_reduce(gs.rearrange("p t g -> p (t g)"), pairs[:, gw, :], AXX, ALU.max))

            def choose(c):
                tw = slice(c * CT, (c + 1) * CT)
                s4 = biased[:, tw, :].rearrange("p t (g e) -> p (t g) e", g=GROUPS)
                gs = gscore[:, tw, :]
                settle()
                other = gs.unsqueeze(2).broadcast_to([P, CT, GROUPS, GROUPS])
                own = gs.unsqueeze(3).broadcast_to([P, CT, GROUPS, GROUPS])
                then(V.tensor_tensor(beats[:, tw], other, own, ALU.is_gt))
                link(V.tensor_tensor(ties[:, tw], other, own, ALU.is_equal))
                link(V.tensor_tensor(ties[:, tw], ties[:, tw],
                                     lower_group[:].unsqueeze(1).broadcast_to([P, CT, GROUPS, GROUPS]), ALU.mult))
                link(V.tensor_tensor(beats[:, tw], beats[:, tw], ties[:, tw], ALU.add))
                link(V.tensor_reduce(grank[:, tw, :], beats[:, tw], AXX, ALU.add))
                link(V.scalar_tensor_tensor(
                    out=masked[:, tw, :].rearrange("p t (g e) -> p (t g) e", g=GROUPS),
                    in0=grank[:, tw, :].rearrange("p t g -> p (t g)").unsqueeze(2).broadcast_to([P, CT * GROUPS, GE]),
                    scalar=2.0, in1=s4, op0=ALU.is_lt, op1=ALU.mult))
                link(V.tensor_scalar(masked[:, tw, :], masked[:, tw, :], 0.0, None, ALU.add))
                for t in range(c * CT, (c + 1) * CT):
                    then(V.max(top[:, t, :], masked[:, t, :]))
                settle()
                for t in range(c * CT, (c + 1) * CT):
                    then(V.max_index(top_i[:, t, :], top[:, t, :], masked[:, t, :]))
                settle()
                for k in range(K2):
                    then(V.tensor_tensor(hit[:, k, tw, :], expert_no[:].unsqueeze(1).broadcast_to([P, CT, E2]),
                                         top_i[:, tw, k:k + 1].broadcast_to([P, CT, E2]), ALU.is_equal))
                settle()
                V.tensor_tensor(chosen[:, tw, :], hit[:, 0, tw, :], hit[:, 1, tw, :], ALU.add
                                ).then_inc(chosen_ready, 1)

            def weigh(c):
                tw = slice(c * CT, (c + 1) * CT)
                link(V.tensor_tensor(cand[:, :, tw, :], hit[:, :, tw, :],
                                     SC[:, tw, :].unsqueeze(1).broadcast_to([P, K2, CT, E2]), ALU.mult))
                link(V.tensor_reduce(pv[:, :, tw], cand[:, :, tw, :], AXX, ALU.add))
                link(V.scalar_tensor_tensor(out=psum_w[:, tw], in0=pv[:, 0, tw], scalar=1.0, in1=pv[:, 1, tw],
                                            op0=ALU.mult, op1=ALU.add))
                link(V.tensor_scalar(psum_w[:, tw], psum_w[:, tw], 1e-20, None, ALU.add))
                link(V.reciprocal(psum_w[:, tw], psum_w[:, tw]))
                for k in range(K2):
                    then(V.tensor_tensor(rows_v[:, tw, k, D], pv[:, k, tw], psum_w[:, tw], ALU.mult))

            dve.wait_ge(x_in[0], 16)
            norm(0)
            w_lo(0)
            w_lo(1)
            encode(0)
            x_lo(0, U_X[0])
            w_lo(2)
            w_lo(3)
            dve.wait_ge(x_in[1], 16)
            norm(1)
            step(0)
            x_lo(1, U_X[1])
            step(1)
            encode(1)
            step(2)
            split_lo(U_RW, RWhi[:], RWlo[:])
            step(3)
            step(4)
            add_back(0)
            norm(0)
            step(5)
            x_lo(0, U_X2[0])
            step(6)
            save_logits(0)
            step(7)
            dve.wait_ge(bias_in, 16)
            dve.wait_ge(consts, CONSTS)
            score_groups(0)
            add_back(1)
            norm(1)
            choose(0)
            x_lo(1, U_X2[1])
            weigh(0)
            save_logits(1)
            score_groups(1)
            choose(1)
            weigh(1)
            rank_bank = misc[U_RANK % 2]
            dve.wait_ge(moved, U_RANK + 1)
            link(V.tensor_copy(count[:], rank_bank[:, NT * E2:(NT + 1) * E2]))
            link(V.tensor_tensor(over[:], count[:].unsqueeze(2).broadcast_to([P, E2, NT]),
                                 starts[:].unsqueeze(1).broadcast_to([P, E2, NT]), ALU.is_gt))
            link(V.tensor_reduce(tiles_of[:], over[:], AXX, ALU.add))
            link(V.tensor_tensor_scan(tiles_to[:], ones_f[:], tiles_of[:], 0.0, ALU.mult, ALU.add))
            link(V.tensor_tensor(first[:], tiles_to[:], tiles_of[:], ALU.subtract))
            link(V.tensor_scalar(first[:], first[:], float(P), None, ALU.mult))
            V.tensor_tensor(place[:], rank_bank[:, 0:NT * E2].rearrange("p (t e) -> p t e", e=E2),
                            first[:].unsqueeze(1).broadcast_to([P, NT, E2]), ALU.add).then_inc(misc_free, 1)
            dve.wait_ge(misc_free, U_RANK + 1)
            link(V.tensor_tensor(cand[:], hit[:], place[:].unsqueeze(1).broadcast_to([P, K2, NT, E2]), ALU.mult))
            link(V.tensor_reduce(spot[:], cand[:], AXX, ALU.add))
            V.tensor_copy(spot_i[:], spot[:]).then_inc(spots_ready, 1)
            link(V.tensor_tensor(past, tiles_to[0:1, :].unsqueeze(1).broadcast_to([1, 32, E2]),
                                 tile_no[:].unsqueeze(2).broadcast_to([1, 32, E2]), ALU.is_le))
            link(V.tensor_reduce(texp[:], past, AXX, ALU.add))
            V.tensor_scalar(texp_i[:], texp[:], float(E2 - 1), None, ALU.min).then_inc(texp_ready, 1)

            def add_shared(t):
                dve.wait_ge(sd_ready, t + 1)
                V.tensor_tensor(X[:, t, :], YT[t % 2][:, 0:D], X[:, t, :], ALU.add).then_inc(sd_added, 1)

            for n in range(NBLK, NBLK + SB):
                shared_act(n)
            for n in range(NBLK, NBLK + SB):
                act_lo(n)
            for n in range(NBLK + SB, NBLK + 2 * SB):
                shared_act(n)
            for n in range(NBLK + SB, NBLK + 2 * SB):
                act_lo(n)
            for t in range(CT):
                add_shared(t)
            for t in range(CT, NT):
                add_shared(t)

            def slot_meta(base, k):
                n = base + k
                dve.wait_ge(xs_in[k % NXS], NXS * n + (16 - NXS * (k % NXS)))
                V.tensor_copy(meta[:, bass.ds(2 * n, 2)], XS[:, k % NXS, D:D + 2].bitcast(I32)
                              ).then_inc(meta_ready, 1)

            def slot_act(base, k):
                n = base + k
                dve.wait_ge(r_ready, n + 1)
                dve.wait_ge(meta_ready, n + 1)
                if not (isinstance(base, int) and n < 2):
                    dve.wait_ge(at_ready, n - 1)
                V.scalar_tensor_tensor(out=A[:, k % 2, :], in0=R[:, k % 2, :],
                                       scalar=meta[:, bass.ds(2 * n, 1)].bitcast(F32),
                                       in1=R[:, k % 2, :], op0=ALU.mult, op1=ALU.mult).then_inc(a_ready, 1)

            def slot_dest(base, k):
                n = base + k
                if not (isinstance(base, int) and n < NXS):
                    dve.wait_ge(y_out[k % NXS], NXS * n - NXS * (k % NXS))
                V.tensor_copy(dest[:, k % NXS:k % NXS + 1], meta[:, bass.ds(2 * n + 1, 1)]).then_inc(dest_ready, 1)

            def slot_save_at(base, k):
                n = base + k
                dve.wait_ge(at_ready, n + 1)
                if not (isinstance(base, int) and n < 2):
                    dve.wait_ge(down_ready, n - 1)
                V.tensor_copy(AT[:, k % 2, :], H[2 + k % 2][:, 0:P]).then_inc(at_saved, 1)

            def slot_step(base, k):
                at = (lambda m: 0 <= base + m < SLOT_TILES) if isinstance(base, int) else (lambda m: True)
                if at(k - 1):
                    slot_save_at(base, k - 1)
                if at(k):
                    slot_act(base, k)
                if at(k - 2):
                    slot_dest(base, k - 2)
                if at(k + 2):
                    slot_meta(base, k + 2)

            slot_meta(0, 0)
            slot_meta(0, 1)
            for n in range(FIRST):
                slot_step(0, n)
            with dve.Fori(0, MAIN) as i:
                for k in range(FIRST, FIRST + NXS):
                    slot_step(NXS * i, k)
            for n in range(AFTER, SLOT_TILES + 2):
                slot_step(0, n)
            for q in range(4):
                tw = slice(2 * q, 2 * q + 2)
                dve.wait_ge(back_in[q], 16)
                link(V.tensor_tensor(X[:, tw, :], X[:, tw, :], back[:, tw, 0:D], ALU.add))
                V.tensor_tensor(X[:, tw, :], X[:, tw, :], back[:, tw, D:2 * D], ALU.add).then_inc(out_ready, 1)


_INS = ["x", "itok_BxS_13_99985", "ctx_2048", "L0_ffn_router_weight", "L0_ffn_e_bias", "L0_ffn_w_up",
        "L0_ffn_w_down", "L0_ffn_shared_up", "L0_ffn_shared_down"]


def kernel(**inputs):
    import numpy as _np
    import concourse.bacc as _bacc
    from concourse import mybir as _mybir
    from concourse.bass_utils import run_bass_kernel_spmd as _run

    nc = _bacc.Bacc("TRN2", target_bir_lowering=False, num_devices=1)
    arrays, args = {}, []
    for name in _INS:
        a = _np.ascontiguousarray(inputs[name])
        arrays[f"in_{name}"] = a
        args.append(nc.dram_tensor(f"in_{name}", a.shape, _mybir.dt.from_np(a.dtype), kind="ExternalInput").ap())
    args.append(nc.dram_tensor("out_0", (4, 256, 256), _mybir.dt.float32, kind="ExternalOutput").ap())
    build(nc, *args)
    r = _run(nc, [arrays], core_ids=[0])
    return r.results[0]["out_0"]
```

```python
import concourse.bass as bass
from concourse import mybir
from contextlib import ExitStack

F32, F32R, BF16, I32 = mybir.dt.float32, mybir.dt.float32r, mybir.dt.bfloat16, mybir.dt.int32
ALU, ACT = mybir.AluOpType, mybir.ActivationFunctionType
AXX = mybir.AxisListType.X

P = 128
TOKENS, D = 1024, 256
KB = D // P
NT = TOKENS // P
CHUNKS, CT = 2, 4
CW = CT * P
E1, F1, VOCAB = 4, 256, 12500
PER_EXPERT = VOCAB // E1
E2, F2, K2 = 16, 128, 2
GROUPS, GE = 4, 4
SH = 512
SB = SH // P
EPS = 1e-5
MARK = (NT - 2, 0)
OUT_PARTS = [(t, t + 1) for t in range(NT)]
EARLY_PARTS = CT
X_PARTS = [(0, 2), (2, CT), (CT, NT)]
ROW = D + 2
SLOT_TILES = (K2 * TOKENS - E2) // P + E2
EARLY_TILES = (K2 * CW - E2) // P + E2
OUT_OF_BOUNDS = 4096
CONSTS = 19
NXS = 4
STEPS = CHUNKS * E1
NBLK = 2 * STEPS
NG = 8
FIRST = 5
UNROLL = 3 * NXS
MAIN = 2
AFTER = FIRST + MAIN * UNROLL


def build(nc, x, token_ids, ctx_w, router_w, e_bias, w_up, w_down, shared_up, shared_down, out):
    ctx = ExitStack()
    with ctx:
        def sb(name, shape, dt=F32):
            return ctx.enter_context(nc.sbuf_tensor(name, shape, dt))

        def sem(name):
            return ctx.enter_context(nc.semaphore(name))

        slots = nc.dram_tensor("slots", [SLOT_TILES * P, ROW], F32, kind="Internal").ap()
        routed = nc.dram_tensor("routed", [K2 * TOKENS, D], F32, kind="Internal").ap()

        X = sb("X", [P, NT, D])
        rows = sb("rows", [P, NT * K2 * ROW])
        rows_v = rows[:, :].rearrange("p (t k r) -> p t k r", t=NT, k=K2)
        back = rows[:, 0:NT * K2 * D].rearrange("p (t r) -> p t r", t=NT)
        XThi = sb("XThi", [P, KB, TOKENS], F32R)
        XTlo = sb("XTlo", [P, KB, TOKENS], F32R)
        ctx_raw = sb("ctx_raw", [P, E1 * KB, D])
        WThi = sb("WThi", [P, E1, KB, F1], F32R)
        WTlo = sb("WTlo", [P, E1, KB, F1], F32R)
        rw_raw = sb("rw_raw", [P, D])
        RWhi = sb("RWhi", [P, KB, P], F32R)
        RWlo = sb("RWlo", [P, KB, P], F32R)
        bias = sb("bias", [P, E2])
        su_raw = sb("su_raw", [P, KB, SH])
        SUhi = sb("SUhi", [P, KB, SH], F32R)
        SUlo = sb("SUlo", [P, KB, SH], F32R)
        sd_raw = sb("sd_raw", [P, SB, D])
        SDhi = sb("SDhi", [P, SB, D], F32R)
        SDlo = sb("SDlo", [P, SB, D], F32R)
        WU = sb("WU", [P, E2 * KB * F2])
        WD = sb("WD", [P, E2 * D])
        ids = sb("ids", [NT, P], I32)
        tile_code = sb("tile_code", [NT, P], BF16)
        code = sb("code", [P, TOKENS], BF16)
        sg = sb("sg", [P, 4, CW])
        sq = sb("sq", [P, 4, CW])
        act1 = sb("act1", [P, 4, CW])
        Ghi = sb("Ghi", [P, NG, CW], F32R)
        Glo = sb("Glo", [P, NG, CW], F32R)
        yTs = sb("yTs", [P, KB, CW])
        logits_T = yTs[0:E2]
        stats = sb("stats", [P, NT, 6])
        mv = sb("mv", [P, NT, 2])
        rstd = sb("rstd", [P, NT])
        shift = sb("shift", [P, NT])
        var = sb("var", [P, NT])
        minus_half_var = sb("minus_half_var", [P, NT])
        half_way = sb("half_way", [P, NT])
        guess = sb("guess", [P, NT], I32)
        XS = sb("XS", [P, NXS, ROW])
        meta = sb("meta", [P, SLOT_TILES * 2], I32)
        XST = sb("XST", [P, 2, D])
        R = sb("R", [P, 2, P])
        AT = sb("AT", [P, 2, P])
        Y = ctx_raw[:, 0:NXS, :]
        WU_now = ctx_raw[:, NXS:NXS + 2, :]
        WD_now = ctx_raw[:, NXS + 2:NXS + 4, :]
        dest = sb("dest", [P, NXS], I32)
        ident = sb("ident", [P, P])
        ident_b = sb("ident_b", [NT, NT], BF16)
        before = sb("before", [P, P], BF16)
        ones = sb("ones", [P, P], BF16)
        lower_group = sb("lower_group", [P, GROUPS, GROUPS])
        expert_no = sb("expert_no", [P, E2])
        starts = sb("starts", [P, NT])
        tile_no = sb("tile_no", [1, 32])
        pad_row = sb("pad_row", [P, ROW])
        ones_f = sb("ones_f", [P, E2])
        SC = sb("SC", [P, NT, E2])
        biased = sb("biased", [P, NT, E2])
        pairs = sb("pairs", [P, NT * GROUPS, 6])
        gscore = sb("gscore", [P, NT, GROUPS])
        beats = sb("beats", [P, NT, GROUPS, GROUPS])
        ties = sb("ties", [P, NT, GROUPS, GROUPS])
        grank = sb("grank", [P, NT, GROUPS])
        masked = sb("masked", [P, NT, E2])
        top = sb("top", [P, NT, 8])
        top_i = sb("top_i", [P, NT, 8], mybir.dt.uint32)
        cand = sb("cand", [P, K2, CT, E2])
        hit = sb("hit", [P, K2, NT, E2])
        chosen = sb("chosen", [P, NT, E2], BF16)
        pv = sb("pv", [P, K2, NT])
        psum_w = sb("psum_w", [P, NT])
        over = sb("over", [P, E2, NT])
        tiles_of = sb("tiles_of", [P, CHUNKS, E2])
        full = sb("full", [P, E2])
        ends = sb("ends", [P, E2 + 1])
        more = sb("more", [P, E2])
        more_to = sb("more_to", [P, E2 + 1])
        on = sb("on", [P, E2])
        all_ends = sb("all_ends", [1, 2 * E2])
        picked = sb("picked", [P, K2, NT, E2])
        place = sb("place", [P, CT, E2])
        beyond = sb("beyond", [P, CT, E2])
        spot = sb("spot", [P, K2, CT])
        spot_i = sb("spot_i", [P, K2, NT], I32)
        past = yTs[0:1].rearrange("p k (n e) -> p (k n) e", e=2 * E2)
        texp = sb("texp", [1, 32])
        second = sb("second", [1, 32])
        texp_i = sb("texp_i", [1, 32], I32)

        misc = [ctx.enter_context(nc.psum_tensor(f"misc{i}", [P, CW], F32)) for i in range(2)]
        H = [ctx.enter_context(nc.psum_tensor(f"H{i}", [P, CW], F32)) for i in range(4)]
        YT = [ctx.enter_context(nc.psum_tensor(f"YT{i}", [P, CW], F32)) for i in range(2)]

        SD_BANKS = [YT[0], YT[1], misc[0], misc[1]]
        W_BANKS = [H[2], H[3], YT[0], YT[1]]

        x_in = [sem(f"x_in{part}") for part in range(len(X_PARTS))]
        ids_in, ctx_in, rw_in, bias_in = sem("ids_in"), [sem(f"ctx_in{h}") for h in range(2)], sem("rw_in"), sem("bias_in")
        su_in, sd_in, wu_in, wd_in = sem("su_in"), sem("sd_in"), sem("wu_in"), sem("wd_in")
        pads_out = sem("pads_out")
        consts = sem("consts")
        dve_chain = sem("dve_chain")
        normed = [sem(f"normed{n}") for n in range(2 * CHUNKS)]
        moved = sem("moved")
        hi_done = sem("hi_done")
        misc_free = sem("misc_free")
        encoded = sem("encoded")
        codes_ready = sem("codes_ready")
        codes_saved = sem("codes_saved")
        w_moved = sem("w_moved")
        whi_done = sem("whi_done")
        wlo_done = sem("wlo_done")
        shi_done = sem("shi_done")
        slo_done = sem("slo_done")
        stats_ready = sem("stats_ready")
        copied = sem("copied")
        h_ready = sem("h_ready")
        sq_done = sem("sq_done")
        act_ready = sem("act_ready")
        ghi_done, glo_done = sem("ghi_done"), sem("glo_done")
        y_done = sem("y_done")
        yT_saved = sem("yT_saved")
        logits_ready = sem("logits_ready")
        logits_saved = sem("logits_saved")
        logits_back = sem("logits_back")
        scored = sem("scored")
        chosen_ready = sem("chosen_ready")
        ranked = sem("ranked")
        spots_ready = sem("spots_ready")
        weighed = sem("weighed")
        texp_ready = sem("texp_ready")
        sd_ready = sem("sd_ready")
        sd_added = sem("sd_added")
        rows_out = sem("rows_out")
        mark_out = sem("mark_out")
        xs_in = [sem(f"xs_in{b}") for b in range(NXS)]
        y_out = [sem(f"y_out{b}") for b in range(NXS)]
        xt_ready, xt_saved = sem("xt_ready"), sem("xt_saved")
        up_picked, down_picked = sem("up_picked"), sem("down_picked")
        up_ready, r_ready, a_ready = sem("up_ready"), sem("r_ready"), sem("a_ready")
        down_ready, y_saved = sem("down_ready"), sem("y_saved")
        meta_ready, dest_ready = sem("meta_ready"), sem("dest_ready")
        scatters_begun = sem("scatters_begun")
        back_in = [sem(f"back_in{q}") for q in range(len(OUT_PARTS))]
        out_ready = sem("out_ready")
        out_done = sem("out_done")

        U_X = [[0, 1], [2, 3]]
        U_RW = 4
        U_BACK = [[5, 6], [7, 8]]
        U_X2 = [[9, 10], [11, 12]]
        SPLITS = [0, 1, 2, 3, 4, 9, 10, 11, 12]

        LOGITS, RANKS = misc[1], misc[0]

        def rank_columns(c):
            at = c * (CT + 1) * E2
            return RANKS[:, at:at + CT * E2], RANKS[:, at + CT * E2:at + (CT + 1) * E2]

        def bank_of(u):
            if u in U_X2[0]:
                return H[U_X2[0].index(u)]
            return YT[U_X2[1].index(u)] if u in U_X2[1] else misc[u % 2]

        x_t = x.rearrange("b (s p) d -> p (b s) d", p=P)
        out_t = out.rearrange("b (s p) d -> p (b s) d", p=P)
        routed_t = routed.rearrange("(t p k) d -> p t (k d)", p=P, k=K2)
        slots_t = slots.rearrange("(n p) r -> n p r", p=P)

        block = ctx.enter_context(nc.Block())

        @block.sync
        def _(sp):
            for part, (t0, t1) in list(enumerate(X_PARTS))[::2]:
                sp.dma_start(X[:, t0:t1, :], x_t[:, t0:t1, :]).then_inc(x_in[part], 16)
            sp.dma_start(ids[:], token_ids.rearrange("b (s p) -> (b s) p", p=P)).then_inc(ids_in, 16)
            sp.dma_start(su_raw[:], shared_up.rearrange("(k p) n -> p k n", p=P)).then_inc(su_in, 16)
            sp.dma_start(sd_raw[:], shared_down.rearrange("(k p) n -> p k n", p=P)).then_inc(sd_in, 16)
            sp.dma_start(WU[:].rearrange("p (e k f) -> p e k f", e=E2, k=KB),
                         w_up.rearrange("e (k p) f -> p e k f", p=P)).then_inc(wu_in, 16)
            sp.dma_start(WD[:].rearrange("p (e d) -> p e d", e=E2),
                         w_down.rearrange("e p d -> p e d")).then_inc(wd_in, 16)
            sp.wait_ge(rows_out, 16 * (K2 * NT - 1))
            sp.wait_ge(mark_out, 16)

            def load(n, rows_of, b):
                if not (isinstance(n, int) and n < NXS):
                    sp.wait_ge(xt_ready, n - NXS + 1)
                    sp.wait_ge(meta_ready, n - NXS + 1)
                sp.dma_start(XS[:, b, :], rows_of).then_inc(xs_in[b], 16)

            for n in range(NXS):
                load(n, slots_t[n], n)
            with sp.Fori(1, SLOT_TILES // NXS) as i:
                for b in range(NXS):
                    load(NXS * i + b, slots[bass.ds(NXS * P * i + b * P, P), :], b)
            for n in range(SLOT_TILES // NXS * NXS, SLOT_TILES):
                load(n, slots_t[n], n % NXS)
            for q, (t0, t1) in enumerate(OUT_PARTS):
                if q <= EARLY_PARTS:
                    tiles = EARLY_TILES + 2 * q if q < EARLY_PARTS else SLOT_TILES
                    for b in range(NXS):
                        sp.wait_ge(y_out[b], 16 * ((tiles - 1 - b) // NXS + 1))
                sp.dma_start(back[:, t0:t1, :], routed_t[:, t0:t1, :]).then_inc(back_in[q], 16)
            for q, (t0, t1) in enumerate(OUT_PARTS[EARLY_PARTS:]):
                sp.wait_ge(out_ready, EARLY_PARTS + q + 1)
                sp.dma_start(out_t[:, t0:t1, :], X[:, t0:t1, :]).then_inc(out_done, 16)
            sp.wait_ge(out_done, 16 * len(OUT_PARTS))
            sp.wait_ge(pads_out, 16)

        @block.gpsimd
        def _(pool):
            n = [0]

            def const(ins):
                n[0] += 1
                ins.then_inc(consts, 1)

            const(pool.memset(rw_raw[:], 0.0))
            const(pool.memset(ends[:, 0:1], 0.0))
            const(pool.memset(more_to[:, 0:1], 0.0))
            const(pool.memset(ident[:], 0.0))
            const(pool.memset(ident_b[:], 0.0))
            const(pool.memset(before[:], 1.0))
            const(pool.memset(lower_group[:], 1.0))
            const(pool.memset(pad_row[:], 0.0))
            const(pool.memset(ones[:], 1.0))
            const(pool.memset(ones_f[:], 1.0))
            pool.wait_ge(consts, n[0])
            const(pool.affine_select(out=ident[:], in_=ident[:], compare_op=ALU.not_equal, fill=1.0, base=0,
                                     pattern=[[-1, P]], channel_multiplier=1))
            const(pool.affine_select(out=ident_b[:], in_=ident_b[:], compare_op=ALU.not_equal, fill=1.0, base=0,
                                     pattern=[[-1, NT]], channel_multiplier=1))
            const(pool.affine_select(out=before[:], in_=before[:], compare_op=ALU.is_gt, fill=0.0, base=0,
                                     pattern=[[1, P]], channel_multiplier=-1))
            const(pool.affine_select(out=lower_group[:], in_=lower_group[:], compare_op=ALU.is_gt, fill=0.0,
                                     base=0, pattern=[[1, GROUPS], [-1, GROUPS]], channel_multiplier=0))
            const(pool.memset(pad_row[:, D + 1:D + 2].bitcast(I32), OUT_OF_BOUNDS))
            const(pool.iota(expert_no[:], pattern=[[1, E2]], base=0, channel_multiplier=0,
                            allow_small_or_imprecise_dtypes=True))
            const(pool.iota(starts[:], pattern=[[P, NT]], base=0, channel_multiplier=0,
                            allow_small_or_imprecise_dtypes=True))
            const(pool.iota(tile_no[:], pattern=[[1, 32]], base=0, channel_multiplier=0,
                            allow_small_or_imprecise_dtypes=True))
            const(pool.iota(rows_v[:, :, :, D + 1:D + 2].bitcast(I32),
                            pattern=[[K2 * P, NT], [1, K2], [0, 1]], base=0, channel_multiplier=K2))
            assert n[0] == CONSTS
            for k, (raw, hi, lo, landed) in enumerate(((su_raw, SUhi, SUlo, su_in), (sd_raw, SDhi, SDlo, sd_in))):
                pool.wait_ge(landed, 16)
                pool.tensor_copy(hi[:], raw[:]).then_inc(shi_done, 1)
                pool.wait_ge(shi_done, k + 1)
                pool.tensor_tensor(lo[:], raw[:], hi[:].bitcast(F32), ALU.subtract).then_inc(slo_done, 1)
            pool.wait_ge(consts, CONSTS)
            pool.wait_ge(wu_in, 16)
            pool.wait_ge(wd_in, 16)
            pool.dma_start(slots.rearrange("(n p) r -> p n r", p=P),
                           pad_row[:].unsqueeze(1).broadcast_to([P, SLOT_TILES, ROW])).then_inc(pads_out, 16)
            for t in range(NT):
                pool.wait_ge(normed[CHUNKS + t // CT], CT)
                pool.tensor_copy(rows_v[:, t, 1, 0:D], rows_v[:, t, 0, 0:D]).then_inc(copied, 1)
            pool.wait_ge(pads_out, 16)
            pool.wait_ge(copied, NT)
            for t in range(NT):
                if t % CT == 0:
                    pool.wait_ge(weighed, K2 * (t // CT + 1))
                    pool.wait_ge(spots_ready, t // CT + 1)
                for k in range(K2):
                    pool.indirect_dma_start(
                        slots, bass.IndirectOffsetOnAxis(ap=spot_i[:, k, t:t + 1], axis=0),
                        rows_v[:, t, k, :], None, bounds_check=SLOT_TILES * P - 1,
                        oob_is_err=False).then_inc(mark_out if (t, k) == MARK else rows_out, 16)

            def scatter(b, n):
                pool.wait_ge(y_saved, n + 1)
                pool.wait_ge(dest_ready, n + 1)
                pool.sem_inc(scatters_begun, 1)
                pool.indirect_dma_start(
                    routed, bass.IndirectOffsetOnAxis(ap=dest[:, b:b + 1], axis=0),
                    Y[:, b, :], None, bounds_check=K2 * TOKENS - 1, oob_is_err=False).then_inc(y_out[b], 16)

            with pool.Fori(0, SLOT_TILES // NXS) as i:
                for b in range(NXS):
                    scatter(b, NXS * i + b)
            for n_ in range(SLOT_TILES // NXS * NXS, SLOT_TILES):
                scatter(n_ % NXS, n_)

        @block.tensor
        def _(pe):
            def use(u):
                if u in U_X2[1]:
                    pe.wait_ge(yT_saved, 4 * CHUNKS)
                elif u in U_X2[0]:
                    pe.wait_ge(sq_done, NBLK)
                elif u >= 2:
                    pe.wait_ge(misc_free, u - 1)
                return bank_of(u)

            def transpose_x(c, kb, u, call):
                bank = use(u)
                pe.wait_ge(normed[call], CT)
                for j in range(CT):
                    last = pe.transpose(bank[:, j * P:(j + 1) * P],
                                        rows_v[:, c * CT + j, 0, kb * P:(kb + 1) * P], ident[:])
                last.then_inc(moved, 1)

            def spread_codes(c):
                pe.wait_ge(wlo_done, c + 1)
                for j in range(CT):
                    t = c * CT + j
                    last = pe.matmul(H[2 + c][:, j * P:(j + 1) * P], ident_b[:, t:t + 1].broadcast_to([NT, P]),
                                     tile_code[:], start=True, stop=True)
                last.then_inc(codes_ready, 1)

            def transpose_w(e):
                for kb in range(KB):
                    for ib in range(KB):
                        last = pe.transpose(W_BANKS[e][:, kb * F1 + ib * P:kb * F1 + (ib + 1) * P],
                                            ctx_raw[:, e * KB + ib, kb * P:(kb + 1) * P], ident[:])
                last.then_inc(w_moved, 1)

            def split_product(dst, pairs_of, sg_check=False):
                terms = [t for (ahi, alo, bhi, blo) in pairs_of for t in ((ahi, bhi), (ahi, blo), (alo, bhi))]
                for j, (a, b) in enumerate(terms):
                    last = pe.matmul(dst, a, b, start=(j == 0), stop=(j == len(terms) - 1))
                return last

            def hidden(s):
                c, e = divmod(s, E1)
                if e == 0:
                    for kb in range(KB):
                        u = SPLITS.index(U_X[c][kb]) + 1
                        pe.wait_ge(hi_done, u)
                        pe.wait_ge(misc_free, U_X[c][kb] + 1)
                pe.wait_ge(whi_done, e + 1)
                pe.wait_ge(wlo_done, e + 1)
                for b in range(2):
                    n = 2 * s + b
                    if n >= 4:
                        pe.wait_ge(sq_done, n - 3)
                    elif n >= 2:
                        pe.wait_ge(codes_saved, n - 1)
                    w = slice(b * P, (b + 1) * P)
                    cw = slice(c * CW, (c + 1) * CW)
                    split_product(H[n % 4][:], [(WThi[:, e, kb, w], WTlo[:, e, kb, w],
                                                 XThi[:, kb, cw], XTlo[:, kb, cw]) for kb in range(KB)]
                                  ).then_inc(h_ready, 1)

            def project(s):
                c, e = divmod(s, E1)
                if e == 0:
                    if c:
                        pe.wait_ge(yT_saved, 4 * c)
                    else:
                        pe.wait_ge(wlo_done, E1)
                for b in range(2):
                    n = 2 * s + b
                    pe.wait_ge(ghi_done, n + 1)
                    pe.wait_ge(glo_done, n + 1)
                    for db in range(KB):
                        w = slice(db * P, (db + 1) * P)
                        g = n % NG
                        terms = ((WThi, Ghi), (WThi, Glo), (WTlo, Ghi))
                        for j, (a, gg) in enumerate(terms):
                            last = pe.matmul(YT[db][:], a[:, e, b, w], gg[:, g, :],
                                             start=(e == 0 and b == 0 and j == 0),
                                             stop=(e == E1 - 1 and b == 1 and j == 2))
                last.then_inc(y_done, 1)

            def transpose_back(c):
                for half in range(2):
                    bank = use(U_BACK[c][half])
                    pe.wait_ge(yT_saved, 4 * c + 2 * half + 2)
                    for j in range(2):
                        for db in range(KB):
                            t = 2 * half + j
                            last = pe.transpose(bank[:, j * D + db * P:j * D + (db + 1) * P],
                                                yTs[:, db, t * P:(t + 1) * P], ident[:])
                    last.then_inc(moved, 1)

            def route(c):
                if c == 0:
                    pe.wait_ge(sq_done, NBLK)
                for u in (U_RW, U_X2[c][1]):
                    pe.wait_ge(hi_done, SPLITS.index(u) + 1)
                    pe.wait_ge(misc_free, u + 1)
                cw = slice(c * CW, (c + 1) * CW)
                split_product(H[2 + c][:], [(RWhi[:, kb, :], RWlo[:, kb, :], XThi[:, kb, cw], XTlo[:, kb, cw])
                                            for kb in range(KB)]).then_inc(logits_ready, 1)

            def route_back(c):
                pe.wait_ge(misc_free, U_BACK[1][0] + 1)
                pe.wait_ge(logits_saved, c + 1)
                for j in range(CT):
                    t = c * CT + j
                    last = pe.transpose(LOGITS[:, t * E2:(t + 1) * E2], logits_T[:, c, j * P:(j + 1) * P],
                                        ident[0:E2, 0:E2])
                last.then_inc(logits_back, 1)

            def rank(c):
                pe.wait_ge(chosen_ready, c + 1)
                pe.wait_ge(misc_free, U_BACK[1][1] + 1)
                t0, t1 = c * CT, (c + 1) * CT
                ranks, counts = rank_columns(c)
                pe.matmul(ranks, before[:], chosen[:, t0:t1, :].rearrange("p t e -> p (t e)"),
                          start=True, stop=False)
                for t in range(t1 - 1):
                    later = max(t + 1, t0)
                    pe.matmul(ranks[:, (later - t0) * E2:CT * E2].rearrange("p (t e) -> p t e", e=E2), ones[:],
                              chosen[:, t:t + 1, :].broadcast_to([P, t1 - later, E2]),
                              start=False, stop=(t == t1 - 2))
                for t in range(t1):
                    last = pe.matmul(counts, ones[:], chosen[:, t, :], start=(t == 0), stop=(t == t1 - 1))
                last.then_inc(ranked, 1)

            def shared_up_blocks(c, blocks):
                for ib in blocks:
                    n = NBLK + SB * c + ib
                    pe.wait_ge(slo_done, 1)
                    pe.wait_ge(misc_free, U_X2[0][1] + 1)
                    if n % 4 >= 2:
                        pe.wait_ge(logits_saved, CHUNKS)
                    pe.wait_ge(sq_done, n - 3)
                    w = slice(ib * P, (ib + 1) * P)
                    cw = slice(c * CW, (c + 1) * CW)
                    split_product(H[n % 4][:], [(SUhi[:, kb, w], SUlo[:, kb, w],
                                                 XThi[:, kb, cw], XTlo[:, kb, cw]) for kb in range(KB)]
                                  ).then_inc(h_ready, 1)

            def shared_down_tiles(c):
                pe.wait_ge(slo_done, 2)
                pe.wait_ge(misc_free, U_X2[1][1] + 1)
                pe.wait_ge(ghi_done, NBLK + SB * (c + 1))
                pe.wait_ge(glo_done, NBLK + SB * (c + 1))
                for j in range(CT):
                    t = c * CT + j
                    if t == NT - 3:
                        pe.wait_ge(mark_out, 16)
                    if t >= 4:
                        pe.wait_ge(sd_added, t - 3)
                    elif t >= 2:
                        pe.wait_ge(spots_ready, CHUNKS)
                    tw = slice(j * P, (j + 1) * P)
                    g = [(NBLK + SB * c + ib) % NG for ib in range(SB)]
                    split_product(SD_BANKS[t % 4][:, 0:D], [(Ghi[:, g[ib], tw], Glo[:, g[ib], tw],
                                                       SDhi[:, ib, :], SDlo[:, ib, :]) for ib in range(SB)]
                                  ).then_inc(sd_ready, 1)

            pe.wait_ge(consts, CONSTS)
            pe.wait_ge(ctx_in[0], 16)
            transpose_w(0)
            transpose_w(1)
            for kb in range(KB):
                transpose_x(0, kb, U_X[0][kb], 0)
            pe.wait_ge(ctx_in[1], 16)
            transpose_w(2)
            pe.wait_ge(encoded, 1)
            for c in range(CHUNKS):
                spread_codes(c)
            transpose_w(3)
            hidden(0)
            hidden(1)
            hidden(2)
            for kb in range(KB):
                transpose_x(1, kb, U_X[1][kb], 1)
            project(0)
            hidden(3)
            project(1)
            bank = use(U_RW)
            pe.wait_ge(rw_in, 16)
            for kb in range(KB):
                last = pe.transpose(bank[:, kb * P:(kb + 1) * P], rw_raw[:, kb * P:(kb + 1) * P], ident[:])
            last.then_inc(moved, 1)
            hidden(4)
            project(2)
            hidden(5)
            project(3)
            hidden(6)
            transpose_back(0)
            project(4)
            hidden(7)
            project(5)
            project(6)
            project(7)
            transpose_back(1)
            for kb in range(KB):
                transpose_x(0, kb, U_X2[0][kb], 2)
            route(0)
            shared_up_blocks(0, (0,))
            route_back(0)
            for kb in range(KB):
                transpose_x(1, kb, U_X2[1][kb], 3)
            shared_up_blocks(0, (1,))
            route(1)
            rank(0)
            route_back(1)
            shared_up_blocks(0, (2, 3))
            shared_up_blocks(1, (0,))
            rank(1)
            shared_up_blocks(1, (1, 2, 3))
            shared_down_tiles(0)
            shared_down_tiles(1)

            def slot_transpose(base, k):
                n = base + k
                pe.wait_ge(xs_in[k % NXS], NXS * n + (16 - NXS * (k % NXS)))
                if not (isinstance(base, int) and n < 2):
                    pe.wait_ge(xt_saved, n - 1)
                for kb in range(KB):
                    last = pe.transpose(misc[k % 2][:, kb * P:(kb + 1) * P],
                                        XS[:, k % NXS, kb * P:(kb + 1) * P], ident[:])
                last.then_inc(xt_ready, 1)

            def slot_up(base, k):
                n = base + k
                pe.wait_ge(xt_saved, n + 1)
                pe.wait_ge(up_picked, n + 1)
                if not (isinstance(base, int) and n < 2):
                    pe.wait_ge(r_ready, n - 1)
                for kb in range(KB):
                    last = pe.matmul(H[k % 2][:, 0:P], WU_now[:, k % 2, kb * F2:(kb + 1) * F2],
                                     XST[:, k % 2, kb * P:(kb + 1) * P], start=(kb == 0), stop=(kb == KB - 1))
                last.then_inc(up_ready, 1)

            def slot_down(base, k):
                n = base + k
                pe.wait_ge(a_ready, n + 1)
                pe.wait_ge(down_picked, n + 1)
                if not (isinstance(base, int) and n < 2):
                    pe.wait_ge(y_saved, n - 1)
                pe.matmul(YT[k % 2][:, 0:D], AT[:, k % 2, :], WD_now[:, k % 2, :],
                          start=True, stop=True).then_inc(down_ready, 1)

            pe.wait_ge(sd_added, NT)
            pe.wait_ge(sq_done, NBLK + CHUNKS * SB)

            def slot_step(base, k):
                at = (lambda m: 0 <= base + m < SLOT_TILES) if isinstance(base, int) else (lambda m: True)
                if at(k):
                    slot_up(base, k)
                if at(k - 1):
                    slot_down(base, k - 1)
                if at(k + 2):
                    slot_transpose(base, k + 2)

            slot_transpose(0, 0)
            slot_transpose(0, 1)
            for n in range(FIRST):
                slot_step(0, n)
            with pe.Fori(0, MAIN) as i:
                for k in range(FIRST, FIRST + UNROLL):
                    slot_step(UNROLL * i, k)
            for n in range(AFTER, SLOT_TILES + 1):
                slot_step(0, n)

        @block.scalar
        def _(act):
            t0, t1 = X_PARTS[1]
            act.dma_start(X[:, t0:t1, :], x_t[:, t0:t1, :]).then_inc(x_in[1], 16)
            for h in range(2):
                act.dma_start(ctx_raw[:, h * E1:(h + 1) * E1, :],
                              ctx_w.rearrange("e (b p) d -> p (e b) d", p=P)[:, h * E1:(h + 1) * E1, :]
                              ).then_inc(ctx_in[h], 16)
            act.wait_ge(consts, 1)
            act.dma_start(rw_raw[0:E2, :], router_w).then_inc(rw_in, 16)
            act.dma_start(bias[:], e_bias.rearrange("(o e) -> o e", o=1).broadcast_to([P, E2])
                          ).then_inc(bias_in, 16)

            def split_hi(u, dst):
                act.wait_ge(moved, u + 1)
                src = bank_of(u)[:]
                if len(dst.shape) == 3:
                    src = bank_of(u)[:, 0:dst.shape[1] * dst.shape[2]].rearrange("p (k n) -> p k n", k=dst.shape[1])
                nc.scalar.activation(dst, src, ACT.Copy).then_inc(hi_done, 1)

            def x_hi(c, uses):
                for kb in range(KB):
                    split_hi(uses[kb], XThi[:, kb, c * CW:(c + 1) * CW])

            def take(n, func):
                act.wait_ge(h_ready, n + 1)
                if n >= 4:
                    act.wait_ge(act_ready, n - 3)
                i = nc.scalar.activation(sg[:, n % 4, :], H[n % 4][:], func)
                if func == ACT.Relu:
                    i.then_inc(sq_done, 1)
                    return
                nc.scalar.activation(sq[:, n % 4, :], H[n % 4][:], ACT.Square).then_inc(sq_done, 1)

            def act_hi(n):
                act.wait_ge(act_ready, n + 1)
                if n >= NG:
                    act.wait_ge(y_done, (n - NG) // 2 + 1)
                nc.scalar.activation(Ghi[:, n % NG, :], act1[:, n % 4, :], ACT.Copy).then_inc(ghi_done, 1)

            def take_step(s):
                for b in range(2):
                    take(2 * s + b, ACT.Sigmoid)

            def hi_step(s):
                for b in range(2):
                    act_hi(2 * s + b)

            def save_y(c):
                act.wait_ge(y_done, E1 * (c + 1))
                if c:
                    act.wait_ge(moved, U_BACK[c - 1][1] + 1)
                for half in range(2):
                    w = slice(half * 2 * P, (half + 1) * 2 * P)
                    for db in range(KB):
                        nc.scalar.activation(yTs[:, db, w], YT[db][:, w], ACT.Copy).then_inc(yT_saved, 1)

            def apply_norm(call, tiles=CT):
                c = call % CHUNKS
                act.wait_ge(stats_ready, call + 1)
                for t in range(c * CT, c * CT + tiles):
                    nc.scalar.activation(rows_v[:, t, 0, 0:D], X[:, t, :], ACT.Identity, bias=shift[:, t:t + 1],
                                         scale=rstd[:, t:t + 1]).then_inc(normed[call], 1)

            def w_hi(e):
                act.wait_ge(w_moved, e + 1)
                nc.scalar.activation(WThi[:, e], W_BANKS[e][:].rearrange("p (k n) -> p k n", k=KB),
                                     ACT.Copy).then_inc(whi_done, 1)

            def save_logits(c):
                act.wait_ge(logits_ready, c + 1)
                act.wait_ge(moved, U_BACK[1][1] + 1)
                nc.scalar.activation(logits_T[:, c, :], H[2 + c][0:E2, :], ACT.Copy).then_inc(logits_saved, 1)

            def scores(c):
                act.wait_ge(logits_back, c + 1)
                nc.scalar.activation(SC[:, c * CT:(c + 1) * CT, :],
                                     LOGITS[:, c * CT * E2:(c + 1) * CT * E2].rearrange("p (t e) -> p t e", e=E2),
                                     ACT.Sigmoid).then_inc(scored, 1)

            def shared_square(n):
                act.wait_ge(sq_done, n + 1)
                act.wait_ge(ghi_done, n - 3)
                act.wait_ge(glo_done, n - 3)
                nc.scalar.activation(act1[:, n % 4, :], sg[:, n % 4, :], ACT.Square).then_inc(act_ready, 1)

            apply_norm(0, 2)
            w_hi(0)
            w_hi(1)
            x_hi(0, U_X[0])
            w_hi(2)
            for c in range(CHUNKS):
                act.wait_ge(codes_ready, c + 1)
                nc.scalar.activation(code[:, c * CW:(c + 1) * CW], H[2 + c][:], ACT.Copy).then_inc(codes_saved, 1)
            take_step(0)
            w_hi(3)
            apply_norm(1)
            hi_step(0)
            take_step(1)
            x_hi(1, U_X[1])
            hi_step(1)
            take_step(2)
            hi_step(2)
            take_step(3)
            split_hi(U_RW, RWhi[:])
            hi_step(3)
            take_step(4)
            take_step(5)
            hi_step(4)
            save_y(0)
            take_step(6)
            hi_step(5)
            hi_step(6)
            take_step(7)
            hi_step(7)
            save_y(1)
            x_hi(0, U_X2[0])
            save_logits(0)
            apply_norm(3, 2)
            scores(0)
            x_hi(1, U_X2[1])
            take(NBLK, ACT.Relu)
            save_logits(1)
            scores(1)
            for n in range(NBLK, NBLK + SB):
                if n > NBLK:
                    take(n, ACT.Relu)
                shared_square(n)
                act_hi(n)
            for n in range(NBLK + SB, NBLK + 2 * SB):
                take(n, ACT.Relu)
                shared_square(n)
                act_hi(n)

            def slot_save_x(base, k):
                n = base + k
                act.wait_ge(xt_ready, n + 1)
                if not (isinstance(base, int) and n < 2):
                    act.wait_ge(up_ready, n - 1)
                nc.scalar.activation(XST[:, k % 2, :], misc[k % 2][:, 0:D], ACT.Copy).then_inc(xt_saved, 1)

            def slot_relu(base, k):
                n = base + k
                act.wait_ge(up_ready, n + 1)
                if not (isinstance(base, int) and n < 2):
                    act.wait_ge(a_ready, n - 1)
                nc.scalar.activation(R[:, k % 2, :], H[k % 2][:, 0:P], ACT.Relu).then_inc(r_ready, 1)

            def slot_save_y(base, k):
                n = base + k
                act.wait_ge(down_ready, n + 1)
                act.wait_ge(meta_ready, n + 1)
                if not (isinstance(base, int) and n < NXS):
                    act.wait_ge(y_out[k % NXS], NXS * n - NXS * (k % NXS))
                nc.scalar.activation(Y[:, k % NXS, :], YT[k % 2][:, 0:D], ACT.Copy,
                                     scale=meta[:, bass.ds(2 * n, 1)].bitcast(F32)).then_inc(y_saved, 1)

            def slot_step(base, k):
                at = (lambda m: 0 <= base + m < SLOT_TILES) if isinstance(base, int) else (lambda m: True)
                if at(k):
                    slot_relu(base, k)
                if at(k - 1):
                    slot_save_y(base, k - 1)
                if at(k + 2):
                    slot_save_x(base, k + 2)

            slot_save_x(0, 0)
            slot_save_x(0, 1)
            for n in range(FIRST):
                slot_step(0, n)
            with act.Fori(0, MAIN) as i:
                for k in range(FIRST, FIRST + UNROLL):
                    slot_step(UNROLL * i, k)
            for n in range(AFTER, SLOT_TILES + 1):
                slot_step(0, n)
            for q, (t0, t1) in enumerate(OUT_PARTS[:EARLY_PARTS]):
                act.wait_ge(out_ready, q + 1)
                act.dma_start(out_t[:, t0:t1, :], X[:, t0:t1, :]).then_inc(out_done, 16)

        @block.vector
        def _(dve):
            chain = [0]

            def then(ins):
                chain[0] += 1
                ins.then_inc(dve_chain, 1)
                return chain[0]

            def after(count):
                dve.wait_ge(dve_chain, count)

            def settle():
                dve.wait_ge(dve_chain, chain[0])

            def link(ins):
                then(ins)
                settle()

            V = nc.vector

            def apply_norm(call, t):
                V.tensor_scalar(rows_v[:, t, 0, 0:D], X[:, t, :], mv[:, t, 0:1], rstd[:, t:t + 1], ALU.subtract,
                                ALU.mult).then_inc(normed[call], 1)

            def norm_stats(t):
                then(V.bn_stats(stats[:, t, :], X[:, t, :]))

            def norm_scale(c):
                settle()
                for t in range(c * CT, (c + 1) * CT):
                    then(V.bn_aggr(mv[:, t, :], stats[:, t, :]))
                settle()
                cs = slice(c * CT, (c + 1) * CT)
                y, z = rstd[:, cs], half_way[:, cs]
                then(V.tensor_scalar(minus_half_var[:, cs], mv[:, cs, 1], EPS, -0.5, ALU.add, ALU.mult))
                link(V.tensor_scalar(var[:, cs], mv[:, cs, 1], EPS, None, ALU.add))
                link(V.tensor_scalar(guess[:, cs], var[:, cs].bitcast(I32), 1, None, ALU.arith_shift_right))
                link(V.tensor_scalar(y.bitcast(I32), guess[:, cs], -1.0, float(0x5F3759DF), ALU.mult, ALU.add))
                link(V.tensor_tensor(var[:, cs], y, y, ALU.mult))
                link(V.tensor_tensor(var[:, cs], var[:, cs], minus_half_var[:, cs], ALU.mult))
                link(V.scalar_tensor_tensor(out=z, in0=var[:, cs], scalar=5 / 3, in1=var[:, cs], op0=ALU.add,
                                            op1=ALU.mult))
                link(V.scalar_tensor_tensor(out=z, in0=z, scalar=1.25, in1=y, op0=ALU.add, op1=ALU.mult))
                link(V.tensor_tensor(var[:, cs], z, z, ALU.mult))
                link(V.scalar_tensor_tensor(out=var[:, cs], in0=var[:, cs], scalar=3.375, in1=minus_half_var[:, cs],
                                            op0=ALU.mult, op1=ALU.mult))
                link(V.scalar_tensor_tensor(out=y, in0=var[:, cs], scalar=2.25, in1=z, op0=ALU.add, op1=ALU.mult))
                V.scalar_tensor_tensor(out=shift[:, cs], in0=mv[:, cs, 0], scalar=-1.0, in1=y, op0=ALU.mult,
                                       op1=ALU.mult).then_inc(stats_ready, 1)

            def w_lo(e):
                dve.wait_ge(whi_done, e + 1)
                V.tensor_tensor(WTlo[:, e], W_BANKS[e][:].rearrange("p (k n) -> p k n", k=KB),
                                WThi[:, e].bitcast(F32), ALU.subtract).then_inc(wlo_done, 1)

            def split_lo(u, hi, lo):
                dve.wait_ge(hi_done, SPLITS.index(u) + 1)
                src = bank_of(u)[:]
                if len(hi.shape) == 3:
                    src = bank_of(u)[:, 0:hi.shape[1] * hi.shape[2]].rearrange("p (k n) -> p k n", k=hi.shape[1])
                V.tensor_tensor(lo, src, hi.bitcast(F32), ALU.subtract).then_inc(misc_free, 1)

            def x_lo(c, uses):
                for kb in range(KB):
                    cw = slice(c * CW, (c + 1) * CW)
                    split_lo(uses[kb], XThi[:, kb, cw], XTlo[:, kb, cw])

            def encode():
                dve.wait_ge(ids_in, 16)
                link(V.tensor_scalar(tile_code[:], ids[:], float(PER_EXPERT), None, ALU.is_ge))
                for e in range(2, E1):
                    link(V.scalar_tensor_tensor(out=tile_code[:], in0=ids[:], scalar=float(e * PER_EXPERT),
                                                in1=tile_code[:], op0=ALU.is_ge, op1=ALU.add))
                dve.sem_inc(encoded, 1)

            def act_lo(n):
                dve.wait_ge(ghi_done, n + 1)
                if n >= NG:
                    dve.wait_ge(y_done, (n - NG) // 2 + 1)
                V.tensor_tensor(Glo[:, n % NG, :], act1[:, n % 4, :], Ghi[:, n % NG, :].bitcast(F32),
                                ALU.subtract).then_inc(glo_done, 1)

            def act_step(s):
                c, e = divmod(s, E1)
                cw = slice(c * CW, (c + 1) * CW)
                dve.wait_ge(codes_saved, c + 1)
                for b in range(2):
                    n = 2 * s + b
                    dve.wait_ge(sq_done, n + 1)
                    then(V.scalar_tensor_tensor(out=sg[:, n % 4, :], in0=code[:, cw], scalar=float(e),
                                                in1=sg[:, n % 4, :], op0=ALU.is_equal, op1=ALU.mult))
                settle()
                for b in range(2):
                    n = 2 * s + b
                    if n >= 4:
                        dve.wait_ge(ghi_done, n - 3)
                        dve.wait_ge(glo_done, n - 3)
                    V.tensor_tensor(act1[:, n % 4, :], sg[:, n % 4, :], sq[:, n % 4, :],
                                    ALU.mult).then_inc(act_ready, 1)

            def lo_step(s):
                for b in range(2):
                    act_lo(2 * s + b)

            def add_back(c):
                for half in range(2):
                    u = U_BACK[c][half]
                    t = c * CT + 2 * half
                    dve.wait_ge(moved, u + 1)
                    V.tensor_tensor(X[:, t:t + 2, :].rearrange("p t d -> p (t d)"), misc[u % 2][:],
                                    X[:, t:t + 2, :].rearrange("p t d -> p (t d)"), ALU.add).then_inc(misc_free, 1)
                dve.wait_ge(misc_free, U_BACK[c][1] + 1)

            def add_shared(t):
                dve.wait_ge(sd_ready, t + 1)
                V.tensor_tensor(X[:, t, :], SD_BANKS[t % 4][:, 0:D], X[:, t, :], ALU.add).then_inc(sd_added, 1)

            def choose_groups(c):
                tw = slice(c * CT, (c + 1) * CT)
                gw = slice(c * CT * GROUPS, (c + 1) * CT * GROUPS)
                dve.wait_ge(scored, c + 1)
                link(V.tensor_tensor(biased[:, tw], SC[:, tw], bias[:].unsqueeze(1).broadcast_to([P, CT, E2]),
                                     ALU.add))
                s4 = biased[:, tw].rearrange("p t (g e) -> p (t g) e", g=GROUPS)
                then(V.tensor_tensor(pairs[:, gw, 0:3], s4[:, :, 0:3], s4[:, :, 1:4], ALU.add))
                then(V.tensor_tensor(pairs[:, gw, 3:5], s4[:, :, 0:2], s4[:, :, 2:4], ALU.add))
                link(V.tensor_tensor(pairs[:, gw, 5:6], s4[:, :, 0:1], s4[:, :, 3:4], ALU.add))
                link(V.tensor_reduce(gscore[:, tw].rearrange("p t g -> p (t g)"), pairs[:, gw], AXX, ALU.max))
                other = gscore[:, tw].unsqueeze(2).broadcast_to([P, CT, GROUPS, GROUPS])
                own = gscore[:, tw].unsqueeze(3).broadcast_to([P, CT, GROUPS, GROUPS])
                then(V.tensor_tensor(ties[:, tw], other, own, ALU.is_equal))
                beaten = then(V.tensor_tensor(beats[:, tw], other, own, ALU.is_gt))
                after(beaten - 1)
                link(V.tensor_tensor(ties[:, tw], ties[:, tw],
                                     lower_group[:].unsqueeze(1).broadcast_to([P, CT, GROUPS, GROUPS]), ALU.mult))
                link(V.tensor_tensor(beats[:, tw], beats[:, tw], ties[:, tw], ALU.add))
                link(V.tensor_reduce(grank[:, tw], beats[:, tw], AXX, ALU.add))
                then(V.scalar_tensor_tensor(
                    out=masked[:, tw].rearrange("p t (g e) -> p (t g) e", g=GROUPS),
                    in0=grank[:, tw].rearrange("p t g -> p (t g)").unsqueeze(2).broadcast_to([P, CT * GROUPS, GE]),
                    scalar=2.0, in1=s4, op0=ALU.is_lt, op1=ALU.mult))

            def choose_experts(c):
                tw = slice(c * CT, (c + 1) * CT)
                settle()
                link(V.tensor_scalar(masked[:, tw], masked[:, tw], 0.0, None, ALU.add))
                tiles = range(c * CT, (c + 1) * CT)
                best = [then(V.max(top[:, t, :], masked[:, t, :])) for t in tiles]
                for t, found in zip(tiles, best):
                    after(found)
                    then(V.max_index(top_i[:, t, :], top[:, t, :], masked[:, t, :]))
                settle()
                for k in range(K2):
                    then(V.tensor_tensor(hit[:, k, tw], expert_no[:].unsqueeze(1).broadcast_to([P, CT, E2]),
                                         top_i[:, tw, k:k + 1].broadcast_to([P, CT, E2]), ALU.is_equal))
                settle()
                V.tensor_tensor(chosen[:, tw], hit[:, 0, tw], hit[:, 1, tw], ALU.add).then_inc(chosen_ready, 1)

            def weigh_and_place(c):
                tw = slice(c * CT, (c + 1) * CT)
                w = then(V.tensor_tensor(picked[:, :, tw], hit[:, :, tw],
                                         SC[:, tw].unsqueeze(1).broadcast_to([P, K2, CT, E2]), ALU.mult))
                after(w)
                w = then(V.tensor_reduce(pv[:, :, tw], picked[:, :, tw], AXX, ALU.add))
                after(w)
                w = then(V.tensor_tensor(psum_w[:, tw], pv[:, 0, tw], pv[:, 1, tw], ALU.add))
                rank_bank, counts = rank_columns(c)
                ranks = rank_bank.rearrange("p (t e) -> p t e", e=E2)
                dve.wait_ge(ranked, c + 1)
                s = then(V.tensor_tensor(over[:], counts.unsqueeze(2).broadcast_to([P, E2, NT]),
                                         starts[:].unsqueeze(1).broadcast_to([P, E2, NT]), ALU.is_gt))
                after(w)
                w = then(V.tensor_scalar(psum_w[:, tw], psum_w[:, tw], 1e-20, None, ALU.add))
                after(s)
                s = then(V.tensor_reduce(tiles_of[:, c], over[:], AXX, ALU.add))
                after(w)
                w = then(V.reciprocal(psum_w[:, tw], psum_w[:, tw]))
                after(s)
                if c == 0:
                    s = then(V.tensor_tensor_scan(ends[:, 1:E2 + 1], ones_f[:], tiles_of[:, 0], 0.0,
                                                  ALU.mult, ALU.add))
                else:
                    s = then(V.tensor_tensor(more[:], tiles_of[:, 1], tiles_of[:, 0], ALU.subtract))
                after(w)
                for k in range(K2):
                    V.tensor_tensor(rows_v[:, tw, k, D], pv[:, k, tw], psum_w[:, tw], ALU.mult).then_inc(weighed, 1)
                after(s)
                here = then(V.scalar_tensor_tensor(out=place[:], in0=ends[:, 0:E2].unsqueeze(1).broadcast_to([P, CT, E2]),
                                                   scalar=float(P), in1=ranks, op0=ALU.mult, op1=ALU.add))
                if c == 1:
                    s = then(V.tensor_tensor_scan(more_to[:, 1:E2 + 1], ones_f[:], more[:], 0.0, ALU.mult, ALU.add))
                    late = then(V.tensor_tensor(beyond[:], ranks, full[:].unsqueeze(1).broadcast_to([P, CT, E2]),
                                                ALU.is_ge))
                    after(s)
                    s = then(V.scalar_tensor_tensor(out=on[:], in0=more_to[:, 0:E2], scalar=ends[:, E2:E2 + 1],
                                                    in1=ends[:, 1:E2 + 1], op0=ALU.add, op1=ALU.subtract))
                    after(s)
                    link(V.tensor_tensor(beyond[:], beyond[:], on[:].unsqueeze(1).broadcast_to([P, CT, E2]),
                                         ALU.mult))
                    here = then(V.scalar_tensor_tensor(out=place[:], in0=beyond[:], scalar=float(P), in1=place[:],
                                                       op0=ALU.mult, op1=ALU.add))
                after(here)
                link(V.tensor_tensor(cand[:], hit[:, :, tw], place[:].unsqueeze(1).broadcast_to([P, K2, CT, E2]),
                                     ALU.mult))
                link(V.tensor_reduce(spot[:], cand[:], AXX, ALU.add))
                V.tensor_copy(spot_i[:, :, tw], spot[:]).then_inc(spots_ready, 1)
                if c == 0:
                    link(V.tensor_scalar(full[:], tiles_of[:, 0], float(P), None, ALU.mult))

            for part in range(2):
                dve.wait_ge(x_in[part], 16)
                for t in range(*X_PARTS[part]):
                    norm_stats(t)
            norm_scale(0)
            for t in (2, 3):
                apply_norm(0, t)
            encode()
            w_lo(0)
            w_lo(1)
            x_lo(0, U_X[0])
            w_lo(2)
            dve.wait_ge(x_in[2], 16)
            for t in range(CT, NT):
                norm_stats(t)
            norm_scale(1)
            act_step(0)
            w_lo(3)
            lo_step(0)
            act_step(1)
            x_lo(1, U_X[1])
            lo_step(1)
            act_step(2)
            lo_step(2)
            act_step(3)
            split_lo(U_RW, RWhi[:], RWlo[:])
            lo_step(3)
            act_step(4)
            act_step(5)
            lo_step(4)
            add_back(0)
            act_step(6)
            lo_step(5)
            lo_step(6)
            act_step(7)
            norm_stats(0)
            norm_stats(1)
            lo_step(7)
            norm_stats(2)
            norm_stats(3)
            norm_scale(0)
            dve.wait_ge(bias_in, 16)
            dve.wait_ge(consts, CONSTS)
            for t in range(CT):
                apply_norm(2, t)
            add_back(1)
            x_lo(0, U_X2[0])
            for t in range(CT, NT):
                norm_stats(t)
            norm_scale(1)
            for t in (6, 7):
                apply_norm(3, t)
            choose_groups(0)
            x_lo(1, U_X2[1])
            choose_experts(0)
            weigh_and_place(0)
            act_lo(NBLK)
            choose_groups(1)
            choose_experts(1)
            act_lo(NBLK + 1)
            weigh_and_place(1)
            for n in range(NBLK + 2, NBLK + SB + 2):
                act_lo(n)
            then(V.tensor_scalar(all_ends[:, E2:2 * E2], more_to[0:1, 1:E2 + 1], ends[0:1, E2:E2 + 1], None, ALU.add))
            link(V.tensor_copy(all_ends[:, 0:E2], ends[0:1, 1:E2 + 1]))
            link(V.tensor_tensor(past, all_ends[:].unsqueeze(1).broadcast_to([1, 32, 2 * E2]),
                                 tile_no[:].unsqueeze(2).broadcast_to([1, 32, 2 * E2]), ALU.is_le))
            link(V.tensor_reduce(texp[:], past, AXX, ALU.add))
            link(V.tensor_scalar(second[:], texp[:], float(E2), float(-E2), ALU.is_ge, ALU.mult))
            link(V.tensor_tensor(texp[:], texp[:], second[:], ALU.add))
            V.tensor_scalar(texp_i[:], texp[:], float(E2 - 1), None, ALU.min).then_inc(texp_ready, 1)
            for n in range(NBLK + SB + 2, NBLK + 2 * SB):
                act_lo(n)
            for t in range(3):
                add_shared(t)

            def slot_meta(base, k):
                n = base + k
                dve.wait_ge(xs_in[k % NXS], NXS * n + (16 - NXS * (k % NXS)))
                V.tensor_copy(meta[:, bass.ds(2 * n, 2)], XS[:, k % NXS, D:D + 2].bitcast(I32)
                              ).then_inc(meta_ready, 1)

            def slot_act(base, k):
                n = base + k
                dve.wait_ge(r_ready, n + 1)
                if not (isinstance(base, int) and n < 2):
                    dve.wait_ge(down_ready, n - 1)
                V.tensor_tensor(AT[:, k % 2, :], R[:, k % 2, :], R[:, k % 2, :], ALU.mult).then_inc(a_ready, 1)

            def slot_dest(base, k):
                n = base + k
                dve.wait_ge(meta_ready, n + 1)
                if not (isinstance(base, int) and n < NXS):
                    dve.wait_ge(y_out[k % NXS], NXS * n - NXS * (k % NXS))
                V.tensor_copy(dest[:, k % NXS:k % NXS + 1], meta[:, bass.ds(2 * n + 1, 1)]).then_inc(dest_ready, 1)

            def experts(n, count):
                return nc.values_load_multi_w_load_instructions(
                    texp_i[0:1, bass.ds(n, count)], engines=[mybir.EngineType.DVE], min_val=0, max_val=E2 - 1,
                    skip_runtime_bounds_check_because="a count of experts, clamped to E2 - 1 where it is made")[1]

            def pick_up(base, k, e):
                n = base + k
                if not (isinstance(base, int) and n < 2):
                    dve.wait_ge(up_ready, n - 1)
                V.tensor_copy(WU_now[:, k % 2, :], WU[:, bass.ds(e * (KB * F2), KB * F2)]).then_inc(up_picked, 1)

            def pick_down(base, k, e):
                n = base + k
                if not (isinstance(base, int) and n < 2):
                    dve.wait_ge(down_ready, n - 1)
                V.tensor_copy(WD_now[:, k % 2, :], WD[:, bass.ds(e * D, D)]).then_inc(down_picked, 1)

            def slot_picks(base, k, e1, e2):
                at = (lambda m: 0 <= base + m < SLOT_TILES) if isinstance(base, int) else (lambda m: True)
                if at(k + 2):
                    pick_up(base, k + 2, e2)
                    slot_meta(base, k + 2)
                if at(k - 1):
                    slot_dest(base, k - 1)
                if at(k + 1):
                    pick_down(base, k + 1, e1)

            dve.wait_ge(wu_in, 16)
            dve.wait_ge(wd_in, 16)
            dve.wait_ge(texp_ready, 1)
            e = experts(0, FIRST + 2)
            for n in range(2):
                pick_up(0, n, e[n])
            pick_down(0, 0, e[0])
            for t in range(3, NT):
                add_shared(t)
            for n in range(2):
                slot_meta(0, n)
            for n in range(FIRST):
                slot_act(0, n)
                slot_picks(0, n, e[n + 1], e[n + 2])
            with dve.Fori(0, MAIN) as i:
                slot_act(UNROLL * i, FIRST)
                e = experts(UNROLL * i + (FIRST + 1), UNROLL + 1)
                for j in range(UNROLL):
                    if j:
                        slot_act(UNROLL * i, FIRST + j)
                    slot_picks(UNROLL * i, FIRST + j, e[j], e[j + 1])
            slot_act(0, AFTER)
            e = experts(AFTER + 1, SLOT_TILES - AFTER - 1) + (None, None, None)
            for n in range(AFTER, SLOT_TILES + 1):
                if AFTER < n < SLOT_TILES:
                    slot_act(0, n)
                slot_picks(0, n, e[n - AFTER], e[n - AFTER + 1])
            for q, (t0, t1) in enumerate(OUT_PARTS):
                tw = slice(t0, t1)
                dve.wait_ge(back_in[q], 16)
                link(V.tensor_tensor(X[:, tw, :], X[:, tw, :], back[:, tw, 0:D], ALU.add))
                V.tensor_tensor(X[:, tw, :], X[:, tw, :], back[:, tw, D:2 * D], ALU.add).then_inc(out_ready, 1)


_INS = ["x", "itok_BxS_13_99985", "ctx_2048", "L0_ffn_router_weight", "L0_ffn_e_bias", "L0_ffn_w_up",
        "L0_ffn_w_down", "L0_ffn_shared_up", "L0_ffn_shared_down"]


def kernel(**inputs):
    import numpy as _np
    import concourse.bacc as _bacc
    from concourse import mybir as _mybir
    from concourse.bass_utils import run_bass_kernel_spmd as _run

    nc = _bacc.Bacc("TRN2", target_bir_lowering=False, num_devices=1)
    arrays, args = {}, []
    for name in _INS:
        a = _np.ascontiguousarray(inputs[name])
        arrays[f"in_{name}"] = a
        args.append(nc.dram_tensor(f"in_{name}", a.shape, _mybir.dt.from_np(a.dtype), kind="ExternalInput").ap())
    args.append(nc.dram_tensor("out_0", (4, 256, 256), _mybir.dt.float32, kind="ExternalOutput").ap())
    build(nc, *args)
    r = _run(nc, [arrays], core_ids=[0])
    return r.results[0]["out_0"]
```
